# Optimizing a Trainium2 kernel written in Bass

```python
import numpy as np
import jax
import jax.numpy as jnp

def _softmax(x, axis=-1):
    return jax.nn.softmax(x, axis=axis)

def _gelu(x):
    return jax.nn.gelu(x, approximate=True)

def _silu(x):
    return jax.nn.silu(x)

def _sigmoid(x):
    return jax.nn.sigmoid(x)

def _layernorm(x, axis=-1, eps=1e-05):
    m = jnp.mean(x, axis=axis, keepdims=True)
    v = jnp.var(x, axis=axis, keepdims=True)
    return (x - m) / jnp.sqrt(v + eps)

def _scatter_add(tgt, idx, src, axis=0):
    return tgt.at[idx].add(src)

def _segment_sum(src, seg, n):
    return jax.ops.segment_sum(src, seg, n)
kernel_name = 'mk_vit_tower_postln_d1_tok_img1024_r4_4dbc27'

def setup_inputs(seed: int=0):
    np.random.seed(seed)
    _w = jnp.asarray

    def _rec_inputs():
        import jax
        import jax.numpy as jnp
        _rk = jax.random.key(seed)
        x = jax.random.uniform(jax.random.fold_in(_rk, 1), (8, 3, 256, 256), jnp.float32, 0.0, 1)
        return x
    x = _rec_inputs()

    def _L0_tok_setup():
        import jax, jax.numpy as jnp
        import numpy as np
        _GRAY_W = (0.2989, 0.587, 0.114)
        key = jax.random.key(seed)
        x = jax.random.uniform(key, (32, 3, 256, 256), dtype=jnp.float32)
        sx = jnp.array([[-3.0, 0.0, 3.0], [-10.0, 0.0, 10.0], [-3.0, 0.0, 3.0]], dtype=jnp.float32)
        scharr = jnp.stack([sx, sx.T])[:, None, :, :]
        return {'x': x, 'scharr': scharr}
    _L0_tok_all = _L0_tok_setup()
    _L0_tok_in = {k: v for k, v in _L0_tok_all.items() if k in ('scharr',)}
    del _L0_tok_all

    def _L0_attn_setup():
        import jax, jax.numpy as jnp
        import numpy as np
        D = 256
        key = jax.random.key(seed)
        ks = jax.random.split(key, 7)
        s = 1.0 / np.sqrt(D)
        X = jax.random.normal(ks[0], (4, 512, D), dtype=jnp.float32)
        Wq = jax.random.uniform(ks[1], (D, D), jnp.float32, -s, s)
        Wk = jax.random.uniform(ks[2], (D, D), jnp.float32, -s, s)
        Wv = jax.random.uniform(ks[3], (D, D), jnp.float32, -s, s)
        bq = jax.random.uniform(ks[4], (D,), jnp.float32, -s, s)
        bk = jax.random.uniform(ks[5], (D,), jnp.float32, -s, s)
        bv = jax.random.uniform(ks[6], (D,), jnp.float32, -s, s)
        return {'X': X, 'Wq': Wq, 'bq': bq, 'Wk': Wk, 'bk': bk, 'Wv': Wv, 'bv': bv}
    _L0_attn_all = _L0_attn_setup()
    _L0_attn_in = {k: v for k, v in _L0_attn_all.items() if k in ('Wq', 'bq', 'Wk', 'bk', 'Wv', 'bv')}
    del _L0_attn_all

    def _L0_ffn_setup():
        import jax, jax.numpy as jnp
        import numpy as np
        N_EXPERTS = 8
        CAP_FACTOR = 1.25
        BATCH, SEQ, DMODEL, DFF = (4, 512, 256, 1024)
        key = jax.random.key(seed)
        k0, k1, k2, k3 = jax.random.split(key, 4)
        x = jax.random.normal(k0, (BATCH, SEQ, DMODEL), dtype=jnp.float32)
        Wr = jax.random.normal(k1, (DMODEL, N_EXPERTS), dtype=jnp.float32) * 0.02
        W1 = jax.random.normal(k2, (N_EXPERTS, DMODEL, DFF), dtype=jnp.float32) * 0.02
        W2 = jax.random.normal(k3, (N_EXPERTS, DFF, DMODEL), dtype=jnp.float32) * 0.02
        return {'x': x, 'Wr': Wr, 'W1': W1, 'W2': W2}
    _L0_ffn_all = _L0_ffn_setup()
    _L0_ffn_in = {k: v for k, v in _L0_ffn_all.items() if k in ('Wr', 'W1', 'W2')}
    del _L0_ffn_all
    return {'x': x, 'L0_tok_scharr': _L0_tok_in['scharr'], 'L0_attn_Wq': _L0_attn_in['Wq'], 'L0_attn_bq': _L0_attn_in['bq'], 'L0_attn_Wk': _L0_attn_in['Wk'], 'L0_attn_bk': _L0_attn_in['bk'], 'L0_attn_Wv': _L0_attn_in['Wv'], 'L0_attn_bv': _L0_attn_in['bv'], 'L0_ffn_Wr': _L0_ffn_in['Wr'], 'L0_ffn_W1': _L0_ffn_in['W1'], 'L0_ffn_W2': _L0_ffn_in['W2']}

def reference(x, L0_tok_scharr, L0_attn_Wq, L0_attn_bq, L0_attn_Wk, L0_attn_bk, L0_attn_Wv, L0_attn_bv, L0_ffn_Wr, L0_ffn_W1, L0_ffn_W2):
    import jax
    import jax.numpy as jnp

    def _L0_tok_ref(x, scharr):
        import jax, jax.numpy as jnp
        import numpy as np
        _GRAY_W = (0.2989, 0.587, 0.114)
        w = jnp.asarray(_GRAY_W, dtype=x.dtype)
        gray = jnp.einsum('bchw,c->bhw', x, w)[:, None]
        edges = jax.lax.conv_general_dilated(gray, scharr, window_strides=(1, 1), padding='SAME', dimension_numbers=('NCHW', 'OIHW', 'NCHW'))
        abs_edges = jnp.sqrt(jnp.square(edges))
        edge = abs_edges.sum(axis=1) / 2
        return edge

    def _L0_attn_ref(X, Wq, bq, Wk, bk, Wv, bv):
        import jax, jax.numpy as jnp
        import numpy as np
        D = 256
        N, S, Dm = X.shape
        scale = jnp.asarray(Dm ** 0.5, X.dtype)
        Q = jnp.einsum('nsd,ed->nse', X, Wq) + bq
        K = jnp.einsum('nsd,ed->nse', X, Wk) + bk
        V = jnp.einsum('nsd,ed->nse', X, Wv) + bv
        scores = jnp.einsum('nqd,nkd->nqk', Q, K) / scale
        causal = jnp.triu(jnp.ones((S, S), dtype=bool), k=1)
        scores = jnp.where(causal, -jnp.inf, scores)
        weights = jax.nn.softmax(scores, axis=-1)
        return jnp.einsum('nqk,nkd->nqd', weights, V)

    def _L0_ffn_ref(x, Wr, W1, W2):
        import jax, jax.numpy as jnp
        import numpy as np
        N_EXPERTS = 8
        CAP_FACTOR = 1.25
        BATCH, SEQ, DMODEL, DFF = (4, 512, 256, 1024)
        B, S, D = x.shape
        E = W1.shape[0]
        cap = int(CAP_FACTOR * B * S / E)
        t = x.reshape(-1, D)
        probs = jax.nn.softmax(t @ Wr, axis=-1)
        idx = jnp.argmax(probs, axis=-1)
        pmax = jnp.max(probs, axis=-1)
        onehot = jax.nn.one_hot(idx, E, dtype=jnp.int32)
        pos = jnp.sum(jnp.cumsum(onehot, axis=0) * onehot, axis=-1) - 1
        kept = pos < cap
        flat = idx * cap + jnp.minimum(pos, cap - 1)
        disp = jnp.zeros((E * cap, D), t.dtype).at[flat].add(t * kept[:, None].astype(t.dtype))
        ein = disp.reshape(E, cap, D)
        h = jax.nn.relu(jnp.einsum('ecd,edf->ecf', ein, W1))
        eout = jnp.einsum('ecf,efd->ecd', h, W2).reshape(E * cap, D)
        comb = jnp.where(kept[:, None], eout[flat], t)
        factor = jnp.where(kept, pmax, jnp.ones_like(pmax))
        out = (comb * factor[:, None]).reshape(B, S, D)
        return out
    h = _L0_tok_ref(x, L0_tok_scharr)
    h = _layernorm(h + _L0_attn_ref(h, L0_attn_Wq, L0_attn_bq, L0_attn_Wk, L0_attn_bk, L0_attn_Wv, L0_attn_bv), axis=-1)
    h = _layernorm(h + _L0_ffn_ref(h, L0_ffn_Wr, L0_ffn_W1, L0_ffn_W2), axis=-1)
    return h

_drawn_inputs = setup_inputs


def setup_inputs(seed=0):
    import zlib

    import numpy as np

    out = dict(_drawn_inputs(seed))
    spreads = {}
    factors = {'L0_attn_bq': 8.0,
     'L0_attn_bk': 8.0,
     'L0_attn_bv': 2.831,
     'L0_ffn_Wr': 2.828,
     'L0_ffn_W1': 3.063}
    for name, (base, spread) in spreads.items():
        noise = np.random.default_rng([zlib.crc32(name.encode()), seed]).standard_normal(out[name].shape)
        drawn = base * np.exp(spread * noise) if base else spread * noise
        out[name] = jnp.asarray(drawn.astype(out[name].dtype))
    for name, factor in factors.items():
        out[name] = (out[name] * factor).astype(out[name].dtype)
    return out
```

```python
from contextlib import ExitStack

import concourse.bass as bass
from concourse import mybir

P = 128
ALU = mybir.AluOpType
ACT = mybir.ActivationFunctionType
AX_X = mybir.AxisListType.X
F32 = mybir.dt.float32
BF16 = mybir.dt.bfloat16
U32 = mybir.dt.uint32

GRAY = (0.2989, 0.587, 0.114)
EPS = 1e-5
MASKED = -3.0e38
CAP_FACTOR = 1.25
NOWHERE = 1 << 20


def vit_tower_kernel(
    nc: bass.Bass,
    x: bass.AP,
    scharr: bass.AP,
    Wq: bass.AP,
    bq: bass.AP,
    Wk: bass.AP,
    bk: bass.AP,
    Wv: bass.AP,
    bv: bass.AP,
    Wr: bass.AP,
    W1: bass.AP,
    W2: bass.AP,
    out: bass.AP,
):
    B, CH, S, D = x.shape
    E, _, F = W1.shape
    DC, SC, FC = D // P, S // P, F // P
    T = B * S
    CAP = int(CAP_FACTOR * T / E)
    TAPS = 3
    BW = P + 4
    BN = P + 2
    ROW = D + 2
    SLOTS = [(i, min(P, CAP - i)) for i in range(0, CAP, P)]
    NS = len(SLOTS)
    SCALE = float(D) ** -0.5
    assert D == 2 * P and S == 2 * P and CH == 3 and F % P == 0

    dispatched = nc.dram_tensor("dispatched", [E * CAP, ROW], F32, kind="Internal").ap()
    out_rows = out.rearrange("b s d -> (b s) d")

    with ExitStack() as ctx:
        def sb(name, shape, dt=F32):
            return ctx.enter_context(nc.sbuf_tensor(name, shape, dt))

        def sem(name):
            return ctx.enter_context(nc.semaphore(name))

        bank = [ctx.enter_context(nc.psum_tensor(f"bank{i}", [P, 512], F32)) for i in range(8)]

        ident = sb("ident", [P, P])
        causal = sb("causal", [P, S])
        tri = sb("tri", [P, P], BF16)
        ones = sb("ones", [P, P], BF16)
        tap_mask = sb("tap_mask", [P, TAPS, BW])
        taps = sb("taps", [P, 2 * TAPS * TAPS])
        half_taps = sb("half_taps", [P, 2 * TAPS * TAPS])
        band = sb("band", [P, TAPS, 2, BW])
        rank = sb("rank", [P, SC, E])
        token_id = sb("token_id", [P, T // P], U32)
        token_idf = sb("token_idf", [P, T // P])
        minus_half = sb("minus_half", [P, 4])
        blank = sb("blank", [P, ROW])
        wq = sb("wq", [P, DC, D])
        wk = sb("wk", [P, DC, D])
        wv = sb("wv", [P, DC, D])
        wvT = sb("wvT", [P, DC, D])
        wqk = sb("wqk", [P, DC, D])
        bqc = sb("bqc", [P, DC])
        bkc = sb("bkc", [P, DC])
        bvb = sb("bvb", [P, D])
        wr = sb("wr", [P, DC, E])
        key_bias = sb("key_bias", [P, DC])
        row_bias = sb("row_bias", [P, DC])
        bias_dot = sb("bias_dot", [P, 1])
        NW = 3
        w1 = sb("w1", [P, NW, DC, F])
        w2 = sb("w2", [P, NW, FC, D])
        pix = sb("pix", [P, 2, CH, SC, D])
        red = sb("red", [P, 2, SC, D])
        gray = sb("gray", [P, 2, SC, D + 2])
        edges_abs = sb("edges_abs", [P, DC, 2, S])
        xT = sb("xT", [P, 2, DC, S])
        xb = sb("xb", [P, 2, SC, D])
        yT = sb("yT", [P, DC, S])
        val = sb("val", [P, 2, SC, D])
        score = sb("score", [P, SC, S])
        rmax = sb("rmax", [P, 2, SC])
        rowc = sb("rowc", [P, SC])
        rowcs = sb("rowcs", [P, SC])
        mrow = sb("mrow", [P, SC])
        nbias = sb("nbias", [P, SC])
        prob = sb("prob", [P, SC, S])
        psumr = sb("psumr", [P, 2, SC])
        rinv = sb("rinv", [P, 2, SC])
        probT = sb("probT", [P, S + P])
        resid = sb("resid", [P, 2, SC, D])
        stats = sb("stats", [P, SC, 6])
        mv = sb("mv", [P, SC, 2])
        ve = sb("ve", [P, SC])
        rstd = sb("rstd", [P, SC])
        nmr = sb("nmr", [P, SC])
        trow = sb("trow", [P, 2, SC, ROW])
        tT = sb("tT", [P, DC, S])
        stats2 = sb("stats2", [P, SC, 6])
        mv2 = sb("mv2", [P, SC, 2])
        ve2 = sb("ve2", [P, SC])
        rstd2 = sb("rstd2", [P, SC])
        sc2 = sb("sc2", [P, SC])
        nmr2 = sb("nmr2", [P, SC])
        lone = sb("lone", [P, 2, SC, D])
        lmax = sb("lmax", [P, SC])
        hit = sb("hit", [P, SC, E])
        hrank = sb("hrank", [P, SC, E])
        best = sb("best", [P, SC])
        onehot = sb("onehot", [P, SC, E], BF16)
        onehots = sb("onehots", [P, B + 1, E], BF16)
        lsub = sb("lsub", [P, SC, E])
        lexp = sb("lexp", [P, SC, E])
        lsum = sb("lsum", [P, SC])
        mine = sb("mine", [P, SC, E])
        place = sb("place", [P, SC])
        over = sb("over", [P, SC])
        base = sb("base", [P, SC])
        slot = sb("slot", [P, 2, SC], U32)
        alone = sb("alone", [P, 2, SC], U32)
        keptn = sb("keptn", [P, SC])
        ein = sb("ein", [P, 2, NS, ROW])
        einT = sb("einT", [P, 2, DC, CAP])
        hT = sb("hT", [P, 3, CAP])
        y = sb("y", [P, 2, NS, D])
        ystats = sb("ystats", [P, NS, 6])
        ymv = sb("ymv", [P, NS, 2])
        yve = sb("yve", [P, NS])
        yrstd = sb("yrstd", [P, NS])
        ynmr = sb("ynmr", [P, NS])
        z = sb("z", [P, 2, NS, D])

        consts_in = sem("consts_in")
        attn_w_in = sem("attn_w_in")
        w_in = [sem(f"w_in{i}") for i in range(NW)]
        pix_in = [sem(f"pix_in{i}") for i in range(2)]
        blanked = sem("blanked")
        rows_out = [sem(f"rows_out{i}") for i in range(2)]
        lone_out = [sem(f"lone_out{i}") for i in range(2)]
        ein_in = [sem(f"ein_in{i}") for i in range(2)]
        z_out = [sem(f"z_out{i}") for i in range(2)]
        pool_const = sem("pool_const")
        pool_step = sem("pool_step")
        dve_step = sem("dve_step")
        dve_const = sem("dve_const")
        band_ready = sem("band_ready")
        setup_mm = sem("setup_mm")
        setup_ev = sem("setup_ev")
        red_ready = sem("red_ready")
        gray_ready = sem("gray_ready")
        conv_done = sem("conv_done")
        edges_ready = sem("edges_ready")
        xT_ready = sem("xT_ready")
        xnat_done = sem("xnat_done")
        y_done = sem("y_done")
        v_done = sem("v_done")
        xb_ready = sem("xb_ready")
        yT_ready = sem("yT_ready")
        val_ready = sem("val_ready")
        scores_done = sem("scores_done")
        nbias_ready = sem("nbias_ready")
        probs_ready = sem("probs_ready")
        pT_done = sem("pT_done")
        probT_ready = sem("probT_ready")
        attn_done = sem("attn_done")
        resid_ready = sem("resid_ready")
        var_ready = sem("var_ready")
        t_ready = sem("t_ready")
        tT_done = sem("tT_done")
        tT_ready = sem("tT_ready")
        logits_done = sem("logits_done")
        lsub_ready = sem("lsub_ready")
        lexp_ready = sem("lexp_ready")
        onehot_ready = sem("onehot_ready")
        count_done = sem("count_done")
        slot_ready = sem("slot_ready")
        factor_ready = sem("factor_ready")
        var2_ready = sem("var2_ready")
        einT_done = sem("einT_done")
        einT_ready = sem("einT_ready")
        h_done = sem("h_done")
        h_ready = sem("h_ready")
        h_used = sem("h_used")
        lone_ready = sem("lone_ready")
        y_ready = sem("y_ready")
        yvar_ready = sem("yvar_ready")
        z_ready = sem("z_ready")

        block = ctx.enter_context(nc.Block())

        N_SMALL = 6
        dispatched_w = dispatched.rearrange("(k p) r -> p k r", p=P)

        @block.sync
        def _(sp):
            def load_pictures(b):
                if b >= 2:
                    sp.wait_ge(gray_ready, b - 1)
                sp.dma_start(pix[:, b % 2].rearrange("p c s d -> p (c s) d"),
                             x[b].rearrange("c (s p) d -> p (c s) d", p=P)).then_inc(pix_in[b % 2], 16)

            load_pictures(0)
            sp.dma_start(taps[:, :], scharr.rearrange("f o a b -> o (f a b)").broadcast_to([P, 2 * TAPS * TAPS])
                         ).then_inc(consts_in, 16)
            sp.dma_start(wq[:, :, :], Wq.rearrange("(p c) d -> p c d", c=DC)).then_inc(attn_w_in, 16)
            sp.dma_start(wk[:, :, :], Wk.rearrange("(p c) d -> p c d", c=DC)).then_inc(attn_w_in, 16)
            sp.dma_start(wv[:, :, :], Wv.rearrange("(c p) d -> p c d", p=P)).then_inc(attn_w_in, 16)
            sp.dma_start(bqc[:, :], bq.rearrange("(p c) -> p c", c=DC)).then_inc(consts_in, 16)
            sp.dma_start(bkc[:, :], bk.rearrange("(p c) -> p c", c=DC)).then_inc(consts_in, 16)
            sp.dma_start(bvb[:, :], bv.rearrange("(o d) -> o d", o=1).broadcast_to([P, D])).then_inc(consts_in, 16)
            sp.dma_start(wr[:, :, :], Wr.rearrange("(c p) e -> p c e", p=P)).then_inc(consts_in, 16)
            load_pictures(1)
            sp.wait_ge(pool_const, 1)
            for k in range(E * CAP // P):
                sp.dma_start(dispatched_w[:, k, :], blank[:, :]).then_inc(blanked, 16)

            def load_expert(e):
                if e >= NW:
                    sp.wait_ge(h_used, FC * (e - NW + 1))
                sp.dma_start(w1[:, e % NW], W1[e].rearrange("(c p) f -> p c f", p=P)).then_inc(w_in[e % NW], 16)
                sp.dma_start(w2[:, e % NW], W2[e].rearrange("(c p) d -> p c d", p=P)).then_inc(w_in[e % NW], 16)

            for b in range(2, B):
                load_pictures(b)
                if b < 2 + NW:
                    load_expert(b - 2)

            def load_rows(e):
                if e >= 2:
                    sp.wait_ge(einT_done, e - 1)
                    sp.wait_ge(y_ready, e - 1)
                    sp.wait_ge(z_out[e % 2], 16 * NS * (e // 2))
                full = CAP // P
                sp.dma_start(ein[:, e % 2, 0:full, :],
                             dispatched[e * CAP:e * CAP + full * P].rearrange("(j p) r -> p j r", p=P)
                             ).then_inc(ein_in[e % 2], 16)
                sp.dma_start(ein[0:CAP - full * P, e % 2, full, :],
                             dispatched[e * CAP + full * P:(e + 1) * CAP]).then_inc(ein_in[e % 2], 16)

            for i in range(2):
                sp.wait_ge(rows_out[i], 16 * SC * (B // 2))
            load_rows(0)
            load_rows(1)
            for e in range(NW, E):
                load_expert(e)
                load_rows(e - 1)
            load_rows(E - 1)
            for i in range(2):
                sp.wait_ge(lone_out[i], 16 * SC * (B // 2))
                sp.wait_ge(z_out[i], 16 * NS * (E // 2))

        @block.gpsimd
        def _(pool):
            steps = [0]

            def link(ins):
                steps[0] += 1
                ins.then_inc(pool_step, 1)
                pool.wait_ge(pool_step, steps[0])

            link(pool.memset(blank[:, :], 0.0))
            pool.memset(blank[:, D + 1:D + 2].bitcast(U32), NOWHERE).then_inc(pool_const, 1)
            link(pool.memset(tap_mask[:, :, :], 0.0))
            link(pool.affine_select(out=tap_mask[:, :, :], in_=tap_mask[:, :, :], compare_op=ALU.not_equal,
                                    fill=1.0, base=-3, pattern=[[1, TAPS], [1, BW]], channel_multiplier=-1))
            pool.memset(gray[:, :, :, :], 0.0).then_inc(pool_const, 1)
            link(pool.memset(ident[:, :], 0.0))
            pool.affine_select(out=ident[:, :], in_=ident[:, :], compare_op=ALU.not_equal, fill=1.0,
                               base=0, pattern=[[-1, P]], channel_multiplier=1).then_inc(pool_const, 1)
            link(pool.memset(causal[:, :], 0.0))
            link(pool.affine_select(out=causal[:, S - P:S], in_=causal[:, S - P:S], compare_op=ALU.is_ge,
                                    fill=MASKED, base=0, pattern=[[-1, P]], channel_multiplier=1))
            link(pool.memset(tri[:, :], 1.0))
            link(pool.affine_select(out=tri[:, :], in_=tri[:, :], compare_op=ALU.is_ge, fill=0.0,
                                    base=0, pattern=[[1, P]], channel_multiplier=-1))
            link(pool.memset(ones[:, :], 1.0))
            link(pool.memset(onehots[:, 0, :], 0.0))
            link(pool.memset(ymv[:, :, :], 1.0))
            link(pool.memset(minus_half[:, :], -0.5))
            link(pool.iota(rank[:, :, :], pattern=[[0, SC], [-1, E]], base=E, channel_multiplier=0,
                           allow_small_or_imprecise_dtypes=True))
            link(pool.iota(token_id[:, :], pattern=[[P, T // P]], base=0, channel_multiplier=1))
            pool.iota(token_idf[:, :], pattern=[[P, T // P]], base=0, channel_multiplier=1,
                      allow_small_or_imprecise_dtypes=True).then_inc(pool_const, 1)

            def norm_rows(b):
                pool.wait_ge(var_ready, b + 1)
                link(pool.tensor_tensor(rstd[:, :], ve[:, :], minus_half[:, 0:SC], ALU.pow))
                link(pool.tensor_tensor(nmr[:, :], mv[:, :, 0], rstd[:, :], ALU.mult))
                link(pool.tensor_scalar(nmr[:, :], nmr[:, :], -1.0, 0.0, ALU.mult, ALU.add))
                if b >= 2:
                    pool.wait_ge(rows_out[b % 2], 16 * SC * (b // 2))
                    pool.wait_ge(tT_done, b - 1)
                link(pool.tensor_copy(trow[:, b % 2, :, D + 1:D + 2].bitcast(U32),
                                      token_id[:, SC * b:SC * b + SC].unsqueeze(2)))
                for s in range(SC):
                    pool.tensor_scalar(trow[:, b % 2, s, 0:D], resid[:, b % 2, s, :], rstd[:, s:s + 1],
                                       nmr[:, s:s + 1], ALU.mult, ALU.add).then_inc(t_ready, 1)
                pool.wait_ge(t_ready, SC * (b + 1))

            def norm_lone(b):
                pool.wait_ge(var2_ready, b + 1)
                link(pool.tensor_tensor(rstd2[:, :], ve2[:, :], minus_half[:, 0:SC], ALU.pow))
                link(pool.tensor_scalar(sc2[:, :], rstd2[:, :], 2.0, 0.0, ALU.mult, ALU.add))
                link(pool.tensor_tensor(nmr2[:, :], mv2[:, :, 0], sc2[:, :], ALU.mult))
                link(pool.tensor_scalar(nmr2[:, :], nmr2[:, :], -1.0, 0.0, ALU.mult, ALU.add))
                if b >= 2:
                    pool.wait_ge(lone_out[b % 2], 16 * SC * (b // 2))
                for s in range(SC):
                    pool.tensor_scalar(lone[:, b % 2, s, :], trow[:, b % 2, s, 0:D], sc2[:, s:s + 1],
                                       nmr2[:, s:s + 1], ALU.mult, ALU.add).then_inc(lone_ready, 1)
                pool.wait_ge(lone_ready, SC * (b + 1))

            def scatter(b):
                pool.wait_ge(slot_ready, b + 1)
                pool.wait_ge(factor_ready, b + 1)
                if b == 0:
                    pool.wait_ge(blanked, 16 * (E * CAP // P))
                for s in range(SC):
                    pool.indirect_dma_start(
                        dispatched, bass.IndirectOffsetOnAxis(ap=slot[:, b % 2, s:s + 1], axis=0),
                        trow[:, b % 2, s, :], None, bounds_check=E * CAP - 1, oob_is_err=False
                    ).then_inc(rows_out[b % 2], 16)
                for s in range(SC):
                    pool.indirect_dma_start(
                        out_rows, bass.IndirectOffsetOnAxis(ap=alone[:, b % 2, s:s + 1], axis=0),
                        lone[:, b % 2, s, :], None, bounds_check=T - 1, oob_is_err=False
                    ).then_inc(lone_out[b % 2], 16)

            for i in range(B + 2):
                if 1 <= i <= B:
                    norm_rows(i - 1)
                    norm_lone(i - 1)
                if 2 <= i:
                    scatter(i - 2)

            def norm_out(e):
                pool.wait_ge(yvar_ready, e + 1)
                link(pool.tensor_tensor(yrstd[:, :], yve[:, :], minus_half[:, 0:NS], ALU.pow))
                link(pool.tensor_tensor(ynmr[:, :], ymv[:, :, 0], yrstd[:, :], ALU.mult))
                link(pool.tensor_scalar(ynmr[:, :], ynmr[:, :], -1.0, 0.0, ALU.mult, ALU.add))
                if e >= 2:
                    pool.wait_ge(z_out[e % 2], 16 * NS * (e // 2))
                for j, (_, n) in enumerate(SLOTS):
                    pool.tensor_scalar(z[0:n, e % 2, j, :], y[0:n, e % 2, j, :], yrstd[0:n, j:j + 1],
                                       ynmr[0:n, j:j + 1], ALU.mult, ALU.add).then_inc(z_ready, 1)
                pool.wait_ge(z_ready, NS * (e + 1))
                for j, (_, n) in enumerate(SLOTS):
                    pool.indirect_dma_start(
                        out_rows,
                        bass.IndirectOffsetOnAxis(ap=ein[0:n, e % 2, j, D + 1:D + 2].bitcast(U32), axis=0),
                        z[0:n, e % 2, j, :], None, bounds_check=T - 1, oob_is_err=False
                    ).then_inc(z_out[e % 2], 16)

            for e in range(E):
                norm_out(e)

        @block.scalar
        def _(act):
            steps = [0]

            def scale_red(b):
                act.wait_ge(pix_in[b % 2], 16 * (b // 2 + 1))
                if b >= 2:
                    act.wait_ge(gray_ready, b - 1)
                act.activation(red[:, b % 2], pix[:, b % 2, 0], ACT.Copy, scale=GRAY[0]).then_inc(red_ready, 1)

            def edges(b):
                if b >= 1:
                    act.wait_ge(xT_ready, b)
                for c in range(DC):
                    act.wait_ge(conv_done, DC * b + c + 1)
                    act.activation(edges_abs[:, c].rearrange("p f s -> p (f s)"), bank[c][:, :], ACT.Abs
                                   ).then_inc(edges_ready, 1)

            def project(b):
                act.wait_ge(y_done, b + 1)
                if b >= 1:
                    act.wait_ge(scores_done, b)
                for c in range(DC):
                    ins = act.activation(yT[:, c, :], bank[3][:, c * S:(c + 1) * S], ACT.Identity,
                                         bias=key_bias[:, c:c + 1])
                ins.then_inc(yT_ready, 1)
                act.wait_ge(v_done, b + 1)
                if b >= 2:
                    act.wait_ge(attn_done, b - 1)
                act.activation(val[:, b % 2].rearrange("p s d -> p (s d)"), bank[4][:, :], ACT.Copy
                               ).then_inc(val_ready, 1)

            def probs(b):
                act.wait_ge(nbias_ready, b + 1)
                if b >= 1:
                    act.wait_ge(pT_done, b)
                if b >= 2:
                    act.wait_ge(resid_ready, b - 1)
                for s in range(SC):
                    n = (s + 1) * P
                    ins = act.activation(prob[:, s, 0:n], score[:, s, 0:n], ACT.Exp, bias=nbias[:, s:s + 1],
                                         scale=SCALE, accum_out=psumr[:, b % 2, s:s + 1])
                ins.then_inc(probs_ready, 1)

            def prob_t(b):
                act.wait_ge(pT_done, b + 1)
                if b >= 1:
                    act.wait_ge(attn_done, b)
                act.activation(probT[:, :], bank[7][:, 0:S + P], ACT.Copy).then_inc(probT_ready, 1)

            def t_t(b):
                act.wait_ge(tT_done, b + 1)
                if b >= 1:
                    act.wait_ge(logits_done, b)
                act.activation(tT[:, :, :].rearrange("p c s -> p (c s)"), bank[2][:, :], ACT.Copy
                               ).then_inc(tT_ready, 1)

            def route_exp(b):
                act.wait_ge(lsub_ready, b + 1)
                act.activation(lexp[:, :, :], lsub[:, :, :], ACT.Exp).then_inc(lexp_ready, 1)

            scale_red(0)
            scale_red(1)
            act.wait_ge(setup_mm, 1)
            for c in range(DC):
                ins = act.activation(wvT[:, c, :], bank[2][:, c * D:(c + 1) * D], ACT.Copy)
            ins.then_inc(setup_ev, 1)
            edges(0)
            act.wait_ge(setup_ev, 3)
            for i in range(B + 1):
                if i >= 1:
                    prob_t(i - 1)
                if i < B:
                    project(i)
                    if i + 2 < B:
                        scale_red(i + 2)
                    probs(i)
                    if i + 1 < B:
                        edges(i + 1)
                if i >= 1:
                    t_t(i - 1)
                    route_exp(i - 1)

            def ein_t(e):
                act.wait_ge(einT_done, e + 1)
                if e >= 2:
                    act.wait_ge(h_done, FC * (e - 1))
                for c, bk_ in enumerate((3, 7)):
                    ins = act.activation(einT[:, e % 2, c, :], bank[bk_][:, 0:CAP], ACT.Copy)
                ins.then_inc(einT_ready, 1)

            def hidden(e, j):
                n = FC * e + j
                act.wait_ge(h_done, n + 1)
                if n >= 3:
                    act.wait_ge(h_used, n - 2)
                act.activation(hT[:, n % 3, :], bank[n % 3][:, 0:CAP], ACT.Relu).then_inc(h_ready, 1)

            ein_t(0)
            for e in range(E):
                for j in range(FC):
                    hidden(e, j)
                    if j == 5 and e + 1 < E:
                        ein_t(e + 1)

        @block.vector
        def _(dve):
            steps = [0]

            def link(ins):
                steps[0] += 1
                ins.then_inc(dve_step, 1)
                dve.wait_ge(dve_step, steps[0])

            dve.wait_ge(consts_in, 16 * 5)
            dve.wait_ge(pool_const, 2)
            link(dve.tensor_scalar(half_taps[:, :], taps[:, :], 0.5, None, ALU.mult))
            for f in range(2):
                for dx in range(TAPS):
                    for dy in range(TAPS):
                        k = (f * TAPS + dy) * TAPS + dx
                        if dy == 0:
                            link(dve.tensor_scalar(band[:, dx, f, :], tap_mask[:, dy, :], half_taps[:, k:k + 1],
                                                   None, ALU.mult))
                        else:
                            ins = dve.scalar_tensor_tensor(band[:, dx, f, :], tap_mask[:, dy, :],
                                                           half_taps[:, k:k + 1], band[:, dx, f, :],
                                                           ALU.mult, ALU.add)
                            if dy < TAPS - 1:
                                link(ins)
                    ins.then_inc(band_ready, 1)

            def make_gray(b):
                dve.wait_ge(red_ready, b + 1)
                if b >= 2:
                    dve.wait_ge(conv_done, DC * (b - 1))
                g = gray[:, b % 2, :, 1:D + 1]
                link(dve.scalar_tensor_tensor(red[:, b % 2], pix[:, b % 2, 1], GRAY[1], red[:, b % 2],
                                              ALU.mult, ALU.add))
                dve.scalar_tensor_tensor(g, pix[:, b % 2, 2], GRAY[2], red[:, b % 2],
                                         ALU.mult, ALU.add).then_inc(gray_ready, 1)

            def tokens(b):
                if b >= 2:
                    dve.wait_ge(scores_done, b - 1)
                dve.wait_ge(edges_ready, DC * (b + 1))
                ins = dve.tensor_tensor(xT[:, b % 2], edges_abs[:, :, 0, :], edges_abs[:, :, 1, :], ALU.add)
                ins.then_inc(xT_ready, 1)

            def residual_in(b):
                dve.wait_ge(xnat_done, b + 1)
                for s in range(SC):
                    ins = dve.tensor_tensor(xb[:, b % 2, s, :], bank[2][:, s * D:(s + 1) * D], bvb[:, :], ALU.add)
                ins.then_inc(xb_ready, 1)

            def softmax_max(b):
                dve.wait_ge(scores_done, b + 1)
                if b >= 1:
                    dve.wait_ge(probs_ready, b)
                link(dve.tensor_scalar(rowc[:, :], bank[7][:, S + P:S + P + SC], bias_dot[:, 0:1], None, ALU.add))
                for s in range(SC):
                    n = (s + 1) * P
                    link(dve.tensor_tensor_reduce(score[:, s, 0:n], bank[6][:, s * S:s * S + n],
                                                  causal[:, S - n:S], 1.0, MASKED, ALU.add, ALU.max,
                                                  rmax[:, b % 2, s:s + 1]))
                link(dve.tensor_tensor(mrow[:, :], rmax[:, b % 2, :], rowc[:, :], ALU.add))
                link(dve.tensor_tensor(mrow[:, :], rowc[:, :], mrow[:, :], ALU.subtract))
                dve.tensor_scalar(nbias[:, :], mrow[:, :], SCALE, None, ALU.mult).then_inc(nbias_ready, 1)

            def softmax_sum(b):
                dve.wait_ge(probs_ready, b + 1)
                link(dve.reciprocal(rinv[:, b % 2, :], psumr[:, b % 2, :]))

            def attend(b):
                dve.wait_ge(attn_done, b + 1)
                if b >= 2:
                    dve.wait_ge(t_ready, SC * (b - 1))
                for s in range(SC):
                    ins = dve.scalar_tensor_tensor(resid[:, b % 2, s, :], bank[5][:, s * D:(s + 1) * D],
                                                   rinv[:, b % 2, s:s + 1], xb[:, b % 2, s, :], ALU.mult, ALU.add)
                    if s < SC - 1:
                        link(ins)
                link2(ins)
                for s in range(SC):
                    link(dve.bn_stats(stats[:, s, :], resid[:, b % 2, s, :]))
                if b >= 1:
                    dve.wait_ge(t_ready, SC * b)
                for s in range(SC):
                    link(dve.bn_aggr(mv[:, s, :], stats[:, s, :]))
                dve.tensor_scalar(ve[:, :], mv[:, :, 1], EPS, None, ALU.add).then_inc(var_ready, 1)

            resids = [0]

            def link2(ins):
                resids[0] += 1
                ins.then_inc(resid_ready, 1)
                dve.wait_ge(resid_ready, resids[0])

            def lone_stats(b):
                dve.wait_ge(t_ready, SC * (b + 1))
                if b >= 1:
                    dve.wait_ge(lone_ready, SC * b)
                for s in range(SC):
                    link(dve.bn_stats(stats2[:, s, :], trow[:, b % 2, s, 0:D]))
                for s in range(SC):
                    link(dve.bn_aggr(mv2[:, s, :], stats2[:, s, :]))
                dve.tensor_scalar(ve2[:, :], mv2[:, :, 1], 4.0, EPS, ALU.mult, ALU.add).then_inc(var2_ready, 1)

            def route(b):
                dve.wait_ge(logits_done, b + 1)
                logits = bank[5][:, 0:SC * E].rearrange("p (s e) -> p s e", e=E)
                link(dve.tensor_reduce(lmax[:, :], logits, AX_X, ALU.max))
                peak = lmax[:, :].unsqueeze(2).broadcast_to([P, SC, E])
                dve.tensor_tensor(lsub[:, :, :], logits, peak, ALU.subtract).then_inc(lsub_ready, 1)
                link(dve.tensor_tensor(hit[:, :, :], logits, peak, ALU.is_equal))
                link(dve.tensor_tensor(hrank[:, :, :], hit[:, :, :], rank[:, :, :], ALU.mult))
                link(dve.tensor_reduce(best[:, :], hrank[:, :, :], AX_X, ALU.max))
                link(dve.tensor_tensor(onehot[:, :, :], rank[:, :, :],
                                       best[:, :].unsqueeze(2).broadcast_to([P, SC, E]), ALU.is_equal))
                link(dve.tensor_tensor(onehots[:, b + 1, :], onehots[:, b, :], onehot[:, 0, :], ALU.add))
                dve.tensor_tensor(onehots[:, b + 1, :], onehots[:, b + 1, :], onehot[:, 1, :], ALU.add
                                  ).then_inc(onehot_ready, 1)
                dve.wait_ge(lexp_ready, b + 1)
                link(dve.tensor_reduce(lsum[:, :], lexp[:, :, :], AX_X, ALU.add))
                dve.reciprocal(trow[:, b % 2, :, D], lsum[:, :]).then_inc(factor_ready, 1)

            def assign(b):
                dve.wait_ge(count_done, b + 1)
                count = bank[5][:, SC * E:2 * SC * E].rearrange("p (s e) -> p s e", e=E)
                link(dve.tensor_tensor(mine[:, :, :], onehot[:, :, :], count, ALU.mult))
                link(dve.tensor_reduce(place[:, :], mine[:, :, :], AX_X, ALU.add))
                link(dve.tensor_scalar(base[:, :], best[:, :], -float(CAP), float(E * CAP - 1), ALU.mult, ALU.add))
                link(dve.tensor_scalar(over[:, :], place[:, :], float(CAP), float(NOWHERE), ALU.is_gt, ALU.mult))
                link(dve.tensor_tensor(base[:, :], base[:, :], place[:, :], ALU.add))
                if b >= 2:
                    dve.wait_ge(rows_out[b % 2], 16 * SC * (b // 2))
                    dve.wait_ge(lone_out[b % 2], 16 * SC * (b // 2))
                link(dve.tensor_tensor(slot[:, b % 2, :], base[:, :], over[:, :], ALU.add))
                link(dve.tensor_scalar(keptn[:, :], over[:, :], -1.0, float(NOWHERE), ALU.mult, ALU.add))
                dve.tensor_tensor(alone[:, b % 2, :], keptn[:, :], token_idf[:, SC * b:SC * b + SC], ALU.add
                                  ).then_inc(slot_ready, 1)

            make_gray(0)
            make_gray(1)
            dve.wait_ge(setup_mm, 2)
            for c in range(DC):
                ins = dve.tensor_copy(wqk[:, c, :], bank[3][:, c * D:(c + 1) * D])
            ins.then_inc(setup_ev, 1)
            link(dve.tensor_copy(key_bias[:, :], bank[4][:, 0:DC]))
            link(dve.tensor_copy(row_bias[:, :], bank[4][:, DC:2 * DC]))
            dve.tensor_copy(bias_dot[:, :], bank[4][:, 2 * DC:2 * DC + 1]).then_inc(setup_ev, 1)
            dve.wait_ge(pool_const, 4)
            tokens(0)
            for i in range(B + 2):
                if i >= 2:
                    assign(i - 2)
                if i < B:
                    residual_in(i)
                if 1 <= i <= B:
                    attend(i - 1)
                if i < B:
                    softmax_max(i)
                    if i + 2 < B:
                        make_gray(i + 2)
                    softmax_sum(i)
                    if i + 1 < B:
                        tokens(i + 1)
                if 1 <= i <= B:
                    lone_stats(i - 1)
                    route(i - 1)

            def expert_out(e):
                dve.wait_ge(h_used, FC * (e + 1))
                if e >= 2:
                    dve.wait_ge(z_ready, NS * (e - 1))
                for j, (_, n) in enumerate(SLOTS):
                    ins = dve.scalar_tensor_tensor(y[0:n, e % 2, j, :], bank[4 + j][0:n, 0:D],
                                                   ein[0:n, e % 2, j, D:D + 1], ein[0:n, e % 2, j, 0:D],
                                                   ALU.mult, ALU.add)
                    if j < NS - 1:
                        link(ins)
                ins.then_inc(y_ready, 1)
                dve.wait_ge(y_ready, e + 1)
                for j, (_, n) in enumerate(SLOTS):
                    link(dve.bn_stats(ystats[0:n, j, :], y[0:n, e % 2, j, :]))
                if e >= 1:
                    dve.wait_ge(z_ready, NS * e)
                for j, (_, n) in enumerate(SLOTS):
                    link(dve.bn_aggr(ymv[0:n, j, :], ystats[0:n, j, :]))
                dve.tensor_scalar(yve[:, :], ymv[:, :, 1], EPS, None, ALU.add).then_inc(yvar_ready, 1)

            for e in range(E):
                expert_out(e)

        @block.tensor
        def _(pe):
            def setup():
                pe.wait_ge(attn_w_in, 16 * 3)
                pe.wait_ge(pool_const, 3)
                for c in range(DC):
                    for k in range(DC):
                        ins = pe.transpose(bank[2][:, c * D + k * P:c * D + (k + 1) * P],
                                           wv[:, k, c * P:(c + 1) * P], ident[:, :])
                ins.then_inc(setup_mm, 1)
                pe.wait_ge(consts_in, 16 * 5)
                for c in range(DC):
                    for k in range(DC):
                        pe.matmul(bank[3][:, c * D:(c + 1) * D], wq[:, k, c * P:(c + 1) * P], wk[:, k, :],
                                  start=(k == 0), stop=(k == DC - 1))
                for c in range(DC):
                    for k in range(DC):
                        pe.matmul(bank[4][:, c:c + 1], wk[:, k, c * P:(c + 1) * P], bqc[:, k:k + 1],
                                  start=(k == 0), stop=(k == DC - 1))
                for c in range(DC):
                    for k in range(DC):
                        pe.matmul(bank[4][:, DC + c:DC + c + 1], wq[:, k, c * P:(c + 1) * P], bkc[:, k:k + 1],
                                  start=(k == 0), stop=(k == DC - 1))
                for k in range(DC):
                    ins = pe.matmul(bank[4][:, 2 * DC:2 * DC + 1], bqc[:, k:k + 1].broadcast_to([P, P]),
                                    bkc[:, k:k + 1], start=(k == 0), stop=(k == DC - 1))
                ins.then_inc(setup_mm, 1)

            def convolve(b):
                pe.wait_ge(gray_ready, b + 1)
                for c in range(DC):
                    if b >= 1:
                        pe.wait_ge(edges_ready, DC * (b - 1) + c + 1)
                    acc = bank[c][:, :].rearrange("p (f s) -> p f s", f=2)
                    for k in range(SC):
                        to = acc[:, :, 0:BN] if k == 0 else acc[:, :, S - BN:S]
                        src = slice(2, 2 + BN) if k == 0 else slice(0, BN)
                        for dx in range(TAPS):
                            ins = pe.matmul(to, gray[:, b % 2, k, c * P + dx:c * P + dx + P],
                                            band[:, dx, :, src], start=(k == 0 and dx == 0),
                                            stop=(k == SC - 1 and dx == TAPS - 1), skip_group_check=True)
                    ins.then_inc(conv_done, 1)

            def project(b):
                pe.wait_ge(xT_ready, b + 1)
                if b >= 1:
                    pe.wait_ge(tT_ready, b - 1) if b >= 2 else None
                for s in range(SC):
                    for c in range(DC):
                        ins = pe.transpose(bank[2][:, s * D + c * P:s * D + (c + 1) * P],
                                           xT[:, b % 2, c, s * P:(s + 1) * P], ident[:, :])
                ins.then_inc(xnat_done, 1)
                if b >= 1:
                    pe.wait_ge(yT_ready, b)
                for c in range(DC):
                    for k in range(DC):
                        ins = pe.matmul(bank[3][:, c * S:(c + 1) * S], wqk[:, k, c * P:(c + 1) * P],
                                        xT[:, b % 2, k, :], start=(k == 0), stop=(k == DC - 1))
                ins.then_inc(y_done, 1)
                if b >= 1:
                    pe.wait_ge(val_ready, b)
                for s in range(SC):
                    for k in range(DC):
                        ins = pe.matmul(bank[4][:, s * D:(s + 1) * D], xT[:, b % 2, k, s * P:(s + 1) * P],
                                        wvT[:, k, :], start=(k == 0), stop=(k == DC - 1))
                ins.then_inc(v_done, 1)

            def scores(b):
                pe.wait_ge(yT_ready, b + 1)
                if b >= 1:
                    pe.wait_ge(nbias_ready, b)
                    pe.wait_ge(probT_ready, b)
                for s in range(SC):
                    for k in range(DC):
                        pe.matmul(bank[7][:, S + P + s:S + P + s + 1], xT[:, b % 2, k, s * P:(s + 1) * P],
                                  row_bias[:, k:k + 1], start=(k == 0), stop=(k == DC - 1))
                for s in range(SC):
                    n = (s + 1) * P
                    for k in range(DC):
                        ins = pe.matmul(bank[6][:, s * S:s * S + n], yT[:, k, s * P:(s + 1) * P],
                                        xT[:, b % 2, k, 0:n], start=(k == 0), stop=(k == DC - 1))
                ins.then_inc(scores_done, 1)

            def prob_t(b):
                pe.wait_ge(probs_ready, b + 1)
                pe.transpose(bank[7][:, 0:P], prob[:, 0, 0:P], ident[:, :])
                pe.transpose(bank[7][:, P:2 * P], prob[:, 1, 0:P], ident[:, :])
                pe.transpose(bank[7][:, 2 * P:3 * P], prob[:, 1, P:2 * P], ident[:, :]).then_inc(pT_done, 1)

            def attend(b):
                pe.wait_ge(probT_ready, b + 1)
                pe.wait_ge(val_ready, b + 1)
                if b >= 1:
                    pe.wait_ge(slot_ready, b)
                pe.matmul(bank[5][:, 0:D], probT[:, 0:P], val[:, b % 2, 0, :], start=True, stop=True)
                pe.matmul(bank[5][:, D:2 * D], probT[:, P:2 * P], val[:, b % 2, 0, :], start=True, stop=False)
                pe.matmul(bank[5][:, D:2 * D], probT[:, 2 * P:3 * P], val[:, b % 2, 1, :], start=False, stop=True
                          ).then_inc(attn_done, 1)

            def turn(b):
                pe.wait_ge(t_ready, SC * (b + 1))
                pe.wait_ge(xb_ready, min(b + 2, B))
                for c in range(DC):
                    for s in range(SC):
                        ins = pe.transpose(bank[2][:, c * S + s * P:c * S + (s + 1) * P],
                                           trow[:, b % 2, s, c * P:(c + 1) * P], ident[:, :])
                ins.then_inc(tT_done, 1)
                pe.wait_ge(tT_ready, b + 1)
                for s in range(SC):
                    for k in range(DC):
                        ins = pe.matmul(bank[5][:, s * E:(s + 1) * E], tT[:, k, s * P:(s + 1) * P], wr[:, k, :],
                                        start=(k == 0), stop=(k == DC - 1))
                ins.then_inc(logits_done, 1)

            def count(b):
                pe.wait_ge(onehot_ready, b + 1)
                o = SC * E
                pe.matmul(bank[5][:, o:o + E], ones[:, :], onehots[:, b, :], start=True, stop=False)
                pe.matmul(bank[5][:, o:o + E], tri[:, :], onehot[:, 0, :], start=False, stop=True)
                pe.matmul(bank[5][:, o + E:o + 2 * E], ones[:, :], onehots[:, b, :], start=True, stop=False)
                pe.matmul(bank[5][:, o + E:o + 2 * E], ones[:, :], onehot[:, 0, :], start=False, stop=False)
                pe.matmul(bank[5][:, o + E:o + 2 * E], tri[:, :], onehot[:, 1, :], start=False, stop=True
                          ).then_inc(count_done, 1)

            setup()
            pe.wait_ge(band_ready, 2 * TAPS)
            convolve(0)
            pe.wait_ge(setup_ev, 3)
            for i in range(B + 2):
                if 1 <= i <= B:
                    prob_t(i - 1)
                if i >= 2:
                    count(i - 2)
                if i < B:
                    project(i)
                if 1 <= i <= B:
                    attend(i - 1)
                if i < B:
                    scores(i)
                    if i + 1 < B:
                        convolve(i + 1)
                if 1 <= i <= B:
                    turn(i - 1)

            def ein_t(e):
                pe.wait_ge(ein_in[e % 2], 32 * (e // 2 + 1))
                if e >= 1:
                    pe.wait_ge(einT_ready, e)
                for c, bk_ in enumerate((3, 7)):
                    for j, (o, n) in enumerate(SLOTS):
                        ins = pe.transpose(bank[bk_][:, o:o + n], ein[0:n, e % 2, j, c * P:(c + 1) * P],
                                           ident[0:n, 0:n])
                ins.then_inc(einT_done, 1)

            def hidden(e, j):
                n = FC * e + j
                if j == 0:
                    pe.wait_ge(w_in[e % NW], 32 * (e // NW + 1))
                    pe.wait_ge(einT_ready, e + 1)
                if n >= 3:
                    pe.wait_ge(h_ready, n - 2)
                for k in range(DC):
                    ins = pe.matmul(bank[n % 3][:, 0:CAP], w1[:, e % NW, k, j * P:(j + 1) * P],
                                    einT[:, e % 2, k, :], start=(k == 0), stop=(k == DC - 1))
                ins.then_inc(h_done, 1)

            def expert_out(e, j):
                n = FC * e + j
                pe.wait_ge(h_ready, n + 1)
                if j == 0 and e >= 1:
                    pe.wait_ge(y_ready, e)
                for i, (o, w) in enumerate(SLOTS):
                    ins = pe.matmul(bank[4 + i][0:w, 0:D], hT[:, n % 3, o:o + w], w2[:, e % NW, j, :],
                                    start=(j == 0), stop=(j == FC - 1))
                ins.then_inc(h_used, 1)

            ein_t(0)
            for e in range(E):
                for j in range(FC):
                    hidden(e, j)
                    if j == 5 and e + 1 < E:
                        ein_t(e + 1)
                    if j >= 2:
                        expert_out(e, j - 2)
                for j in range(FC - 2, FC):
                    expert_out(e, j)


_INS = ['x', 'L0_tok_scharr', 'L0_attn_Wq', 'L0_attn_bq', 'L0_attn_Wk', 'L0_attn_bk', 'L0_attn_Wv', 'L0_attn_bv',
        'L0_ffn_Wr', 'L0_ffn_W1', 'L0_ffn_W2']
_OUTS = [((8, 256, 256), 'float32')]


def kernel(**inputs):
    import numpy as _np
    import concourse.bacc as _bacc
    from concourse import mybir as _mybir
    from concourse.bass_utils import run_bass_kernel_spmd as _run

    nc = _bacc.Bacc("TRN2", target_bir_lowering=False, num_devices=1)
    arrays, args = {}, []
    for name in _INS:
        a = _np.ascontiguousarray(inputs[name])
        arrays[f"in_{name}_dram"] = a
        args.append(nc.dram_tensor(f"in_{name}_dram", a.shape, _mybir.dt.from_np(a.dtype), kind="ExternalInput").ap())
    for i, (shape, dtype) in enumerate(_OUTS):
        dt = _mybir.dt.from_np(_np.dtype(dtype))
        args.append(nc.dram_tensor(f"out_{i}_dram", shape, dt, kind="ExternalOutput").ap())
    vit_tower_kernel(nc, *args)
    r = _run(nc, [arrays], core_ids=[0])
    got = tuple(r.results[0][f"out_{i}_dram"] for i in range(len(_OUTS)))
    return got[0]
```

```python
from contextlib import ExitStack

import concourse.bass as bass
from concourse import mybir

P = 128
ALU = mybir.AluOpType
ACT = mybir.ActivationFunctionType
AX_X = mybir.AxisListType.X
F32 = mybir.dt.float32
F32R = mybir.dt.float32r
BF16 = mybir.dt.bfloat16
U32 = mybir.dt.uint32

GRAY = (0.2989, 0.587, 0.114)
EPS = 1e-5
MASKED = -3.0e38
CAP_FACTOR = 1.25
NOWHERE = 1 << 20


def vit_tower_kernel(
    nc: bass.Bass,
    x: bass.AP,
    scharr: bass.AP,
    Wq: bass.AP,
    bq: bass.AP,
    Wk: bass.AP,
    bk: bass.AP,
    Wv: bass.AP,
    bv: bass.AP,
    Wr: bass.AP,
    W1: bass.AP,
    W2: bass.AP,
    out: bass.AP,
):
    B, CH, S, D = x.shape
    E, _, F = W1.shape
    DC, SC, FC = D // P, S // P, F // P
    T = B * S
    CAP = int(CAP_FACTOR * T / E)
    TAPS = 3
    GR = P // TAPS
    GO = GR - TAPS + 1
    GROUPS = -(-S // GO)
    PAD_ROWS = (GROUPS - 1) * GO + GR
    PAD_COLS = D + TAPS - 1
    ROW = D + 2
    SLOTS = [(i, min(P, CAP - i)) for i in range(0, CAP, P)]
    NS = len(SLOTS)
    SCALE = float(D) ** -0.5
    assert D == 2 * P and S == 2 * P and CH == 3 and F % P == 0

    dispatched = nc.dram_tensor("dispatched", [E * CAP, ROW], F32, kind="Internal").ap()
    padded = nc.dram_tensor("padded", [B, PAD_ROWS, PAD_COLS], F32, kind="Internal").ap()
    out_rows = out.rearrange("b s d -> (b s) d")

    with ExitStack() as ctx:
        def sb(name, shape, dt=F32):
            return ctx.enter_context(nc.sbuf_tensor(name, shape, dt))

        def sem(name):
            return ctx.enter_context(nc.semaphore(name))

        bank = [ctx.enter_context(nc.psum_tensor(f"bank{i}", [P, 512], F32)) for i in range(8)]
        LOGITS, COUNTS, VALUES = 0, SC * E, P

        ident = sb("ident", [P, P])
        causal = sb("causal", [P, S])
        tri = sb("tri", [P, P], BF16)
        ones = sb("ones", [P, P], BF16)
        tap_mask = sb("tap_mask", [P, TAPS, GO])
        TAP_COLS = 2 * TAPS * TAPS - (TAPS - 1)
        taps = sb("taps", [P, TAP_COLS])
        half_taps = sb("half_taps", [P, TAP_COLS])
        band = sb("band", [P, 2, GO])
        rank = sb("rank", [P, SC, E])
        token_id = sb("token_id", [P, T // P], U32)
        minus_half = sb("minus_half", [P, 4])
        zeros = sb("zeros", [32, PAD_COLS])
        blank = sb("blank", [P, ROW])
        wq = sb("wq", [P, DC, D])
        wk = sb("wk", [P, DC, D])
        wv = sb("wv", [P, DC, D])
        wvT = sb("wvT", [P, DC, D + 1])
        wqk = sb("wqk", [P, DC, D])
        bqc = sb("bqc", [P, DC])
        bkc = sb("bkc", [P, DC])
        bvb = sb("bvb", [P, D])
        wr = sb("wr", [P, DC, E])
        key_bias = sb("key_bias", [P, DC])
        bias_dot = sb("bias_dot", [P, 1])
        WCOLS = DC * F + FC * D
        PIECE = WCOLS // 4
        w_raw = sb("w_raw", [P, 2, WCOLS])
        w_hi = sb("w_hi", [P, 2, WCOLS], F32R)
        w_lo = sb("w_lo", [P, 2, WCOLS], F32R)
        PIX, SHIFTED, EIN = 2 * CH * SC * D, 2 * GROUPS * D, E * NS * ROW
        images = sb("images", [P, max(PIX + SHIFTED, EIN)])
        pix = images[:, 0:PIX].rearrange("p (b c s d) -> p b c s d", b=2, c=CH, s=SC)
        red = sb("red", [P, 2, SC, D])
        gray = sb("gray", [P, 2, SC, PAD_COLS])
        shifted = images[0:TAPS * GR, PIX:PIX + SHIFTED].rearrange("p (b g d) -> p b g d", b=2, g=GROUPS)
        tokens_mem = sb("tokens_mem", [P, max(12 * D, 4 * NS * D)])
        edges_abs = tokens_mem[:, 0:4 * D].rearrange("p (c f s) -> p c f s", c=DC, f=2)
        xT = sb("xT", [P, 2, DC, S])
        xb = tokens_mem[:, 4 * D:8 * D].rearrange("p (b s d) -> p b s d", b=2, s=SC)
        yT = tokens_mem[:, 8 * D:10 * D].rearrange("p (c s) -> p c s", c=DC)
        val = sb("val", [P, 2, SC, D])
        score = tokens_mem[:, 10 * D:12 * D].rearrange("p (c s) -> p c s", c=SC)
        nmax = sb("nmax", [P, SC])
        rowc = sb("rowc", [P, SC])
        nfull = sb("nfull", [P, SC])
        nbias = sb("nbias", [P, SC])
        prob = sb("prob", [P, SC, S])
        psumr = sb("psumr", [P, 2, SC])
        rinv = sb("rinv", [P, 2, SC])
        probT = sb("probT", [P, S + P])
        resid = sb("resid", [P, 2, SC, D])
        stats = sb("stats", [P, SC, 6])
        mv = sb("mv", [P, SC, 2])
        ve = sb("ve", [P, SC])
        nmean = sb("nmean", [P, SC])
        rstd = sb("rstd", [P, 2, SC])
        nmr = sb("nmr", [P, 2, SC])
        v2 = sb("v2", [P, SC])
        v2n = sb("v2n", [P, SC])
        v2e = sb("v2e", [P, SC])
        lone_scale = sb("lone_scale", [P, 2, SC])
        TR = 3
        trow = sb("trow", [P, TR, SC, ROW])
        tT = sb("tT", [P, DC, S])
        lone = sb("lone", [P, 2, SC, D])
        lmax = sb("lmax", [P, SC])
        hit = sb("hit", [P, SC, E])
        hrank = sb("hrank", [P, SC, E])
        best = sb("best", [P, 2, SC])
        onehot = sb("onehot", [P, 2, SC, E], BF16)
        onehots = sb("onehots", [P, B + 1, E], BF16)
        lsub = sb("lsub", [P, SC, E])
        lexp = sb("lexp", [P, SC, E])
        lsum = sb("lsum", [P, SC])
        mine = sb("mine", [P, SC, E])
        place = sb("place", [P, SC])
        over = sb("over", [P, SC])
        base = sb("base", [P, SC])
        basep = sb("basep", [P, SC])
        slot = sb("slot", [P, TR, SC], U32)
        ein = images[:, 0:EIN].rearrange("p (e j r) -> p e j r", e=E, j=NS)
        einT_hi = sb("einT_hi", [P, 2, DC, CAP], F32R)
        einT_lo = sb("einT_lo", [P, 2, DC, CAP], F32R)
        h_hi = sb("h_hi", [P, 3, CAP], F32R)
        h_lo = sb("h_lo", [P, 3, CAP], F32R)
        y = tokens_mem[:, 0:2 * NS * D].rearrange("p (b j d) -> p b j d", b=2, j=NS)
        ystats = sb("ystats", [P, NS, 6])
        ymv = sb("ymv", [P, NS, 2])
        yve = sb("yve", [P, NS])
        ynmean = sb("ynmean", [P, NS])
        yrstd = sb("yrstd", [P, 2, NS])
        ynmr = sb("ynmr", [P, 2, NS])
        z = tokens_mem[:, 2 * NS * D:4 * NS * D].rearrange("p (b j d) -> p b j d", b=2, j=NS)

        taps_in = sem("taps_in")
        bias_in = sem("bias_in")
        consts_in = sem("consts_in")
        attn_w_in = sem("attn_w_in")
        w_in = [sem(f"w_in{i}") for i in range(2)]
        pix_in = [sem(f"pix_in{i}") for i in range(2)]
        frame_out = sem("frame_out")
        gray_out = [sem(f"gray_out{i}") for i in range(2)]
        shifted_in = [sem(f"shifted_in{i}") for i in range(2)]
        blanked = sem("blanked")
        rows_out = [sem(f"rows_out{i}") for i in range(TR)]
        lone_out = [sem(f"lone_out{i}") for i in range(2)]
        ein_in = [sem(f"ein_in{i}") for i in range(E)]
        z_out = [sem(f"z_out{i}") for i in range(2)]
        pool_const = sem("pool_const")
        pool_step = sem("pool_step")
        dve_step = sem("dve_step")
        band_ready = sem("band_ready")
        setup_mm = sem("setup_mm")
        setup_ev = sem("setup_ev")
        red_ready = sem("red_ready")
        gray_ready = sem("gray_ready")
        conv_done = sem("conv_done")
        edges_ready = sem("edges_ready")
        xT_ready = sem("xT_ready")
        xnat_done = sem("xnat_done")
        tile_done = sem("tile_done")
        y_done = sem("y_done")
        v_done = sem("v_done")
        xb_ready = sem("xb_ready")
        yT_ready = sem("yT_ready")
        rowc_ready = sem("rowc_ready")
        scores_done = sem("scores_done")
        nmax_ready = sem("nmax_ready")
        nbias_ready = sem("nbias_ready")
        probs_ready = sem("probs_ready")
        pT_done = sem("pT_done")
        probT_ready = sem("probT_ready")
        attn_done = sem("attn_done")
        resid_ready = sem("resid_ready")
        var_ready = sem("var_ready")
        rstd_ready = sem("rstd_ready")
        t_ready = sem("t_ready")
        lone_scale_ready = sem("lone_scale_ready")
        lone_ready = sem("lone_ready")
        tT_done = sem("tT_done")
        tT_ready = sem("tT_ready")
        logits_done = sem("logits_done")
        lsub_ready = sem("lsub_ready")
        lexp_ready = sem("lexp_ready")
        onehot_ready = sem("onehot_ready")
        count_done = sem("count_done")
        slot_ready = sem("slot_ready")
        factor_ready = sem("factor_ready")
        w_hi_ready = sem("w_hi_ready")
        w_lo_ready = sem("w_lo_ready")
        einT_done = sem("einT_done")
        einT_hi_ready = sem("einT_hi_ready")
        einT_ready = sem("einT_ready")
        h_done = sem("h_done")
        h_hi_ready = sem("h_hi_ready")
        h_ready = sem("h_ready")
        h_used = sem("h_used")
        y_ready = sem("y_ready")
        yvar_ready = sem("yvar_ready")
        yrstd_ready = sem("yrstd_ready")
        z_ready = sem("z_ready")

        block = ctx.enter_context(nc.Block())

        dispatched_w = dispatched.rearrange("(k p) r -> p k r", p=P)
        BLANKS = 4
        KB = E * CAP // P // BLANKS
        AHEAD_CONV, AHEAD_GRAY = 2, 4
        SPLIT_AT = 4

        @block.sync
        def _(sp):
            def load_picture(b):
                if b >= 2:
                    sp.wait_ge(gray_ready, b - 1)
                sp.dma_start(pix[:, b % 2].rearrange("p c s d -> p (c s) d"),
                             x[b].rearrange("c (s p) d -> p (c s) d", p=P)).then_inc(pix_in[b % 2], 16)

            def store_gray(b):
                sp.wait_ge(gray_ready, b + 1)
                sp.dma_start(padded[b, 1:1 + S, :].rearrange("(s p) d -> p s d", p=P), gray[:, b % 2]
                             ).then_inc(gray_out[b % 2], 16)

            def load_shifted(b):
                sp.wait_ge(gray_out[b % 2], 16 * (b // 2 + 1))
                if b == 0:
                    sp.wait_ge(frame_out, 32)
                if b >= 2:
                    sp.wait_ge(conv_done, DC * (b - 1))
                for dx in range(TAPS):
                    src = bass.AP(padded.tensor, padded[b, 0, dx].offset,
                                  [[PAD_COLS, GR], [GO * PAD_COLS, GROUPS], [1, D]])
                    sp.dma_start(shifted[dx * GR:(dx + 1) * GR, b % 2], src).then_inc(shifted_in[b % 2], 16)

            def load_first(e):
                if e >= 2:
                    sp.wait_ge(w_lo_ready, 4 * (e - 1))
                sp.dma_start(w_raw[:, e % 2, 0:DC * F].rearrange("p (c f) -> p c f", c=DC),
                             W1[e].rearrange("(c p) f -> p c f", p=P)).then_inc(w_in[e % 2], 16)

            def load_second(e):
                sp.dma_start(w_raw[:, e % 2, DC * F:WCOLS].rearrange("p (c d) -> p c d", c=FC),
                             W2[e].rearrange("(c p) d -> p c d", p=P)).then_inc(w_in[e % 2], 16)

            def store_lone(b):
                sp.wait_ge(lone_ready, b + 1)
                sp.dma_start(out_rows[b * S:(b + 1) * S].rearrange("(s p) d -> p s d", p=P), lone[:, b % 2]
                             ).then_inc(lone_out[b % 2], 16)

            def fill_table(k):
                sp.dma_start(dispatched_w[:, k * KB:(k + 1) * KB, :],
                             blank[:, :].unsqueeze(1).broadcast_to([P, KB, ROW])).then_inc(blanked, 16)

            load_picture(0)
            for dx in range(TAPS):
                src = bass.AP(scharr.tensor, dx, [[0, GR], [1, TAP_COLS]])
                sp.dma_start(taps[dx * GR:(dx + 1) * GR], src).then_inc(taps_in, 16)
            sp.dma_start(wv[:, :, :], Wv.rearrange("(c p) d -> p c d", p=P)).then_inc(attn_w_in, 16)
            sp.dma_start(wq[:, :, :], Wq.rearrange("(p c) d -> p c d", c=DC)).then_inc(attn_w_in, 16)
            sp.dma_start(wk[:, :, :], Wk.rearrange("(p c) d -> p c d", c=DC)).then_inc(attn_w_in, 16)
            sp.dma_start(bqc[:, :], bq.rearrange("(p c) -> p c", c=DC)).then_inc(bias_in, 16)
            sp.dma_start(bkc[:, :], bk.rearrange("(p c) -> p c", c=DC)).then_inc(bias_in, 16)
            sp.wait_ge(pool_const, 1)
            sp.dma_start(padded[:, 0, :], zeros[0:B, :]).then_inc(frame_out, 16)
            sp.dma_start(padded[:, 1 + S:PAD_ROWS, :].rearrange("b r c -> r b c"),
                         zeros[0:PAD_ROWS - 1 - S, :].unsqueeze(1).broadcast_to(
                             [PAD_ROWS - 1 - S, B, PAD_COLS])).then_inc(frame_out, 16)
            store_gray(0)
            load_shifted(0)
            load_picture(1)
            load_picture(2)
            sp.dma_start(bvb[:, :], bv.rearrange("(o d) -> o d", o=1).broadcast_to([P, D])).then_inc(consts_in, 16)
            sp.dma_start(wr[:, :, :], Wr.rearrange("(c p) e -> p c e", p=P)).then_inc(consts_in, 16)
            sp.wait_ge(pool_const, 2)
            for b in range(1, AHEAD_GRAY):
                store_gray(b)
                load_picture(b + 2)
                if b < AHEAD_CONV:
                    load_shifted(b)
            for i in range(B + 2):
                if i >= 0 and i + AHEAD_CONV < B:
                    load_shifted(i + AHEAD_CONV)
                if i < 2:
                    fill_table(2 * i)
                    fill_table(2 * i + 1)
                elif i < 6:
                    load_first((i - 2) // 2) if i % 2 == 0 else load_second((i - 2) // 2)
                if i >= 2:
                    store_lone(i - 2)
                if i + AHEAD_GRAY < B:
                    store_gray(i + AHEAD_GRAY)
                if i + AHEAD_GRAY + 2 < B:
                    load_picture(i + AHEAD_GRAY + 2)

            for i in range(TR):
                sp.wait_ge(rows_out[i], 16 * SC * len(range(i, B, TR)))
            full = CAP // P
            for e in range(E):
                sp.dma_start(ein[:, e, 0:full, :],
                             dispatched[e * CAP:e * CAP + full * P].rearrange("(j p) r -> p j r", p=P)
                             ).then_inc(ein_in[e], 16)
                sp.dma_start(ein[0:CAP - full * P, e, full, :],
                             dispatched[e * CAP + full * P:(e + 1) * CAP]).then_inc(ein_in[e], 16)
            for e in range(2, E):
                load_first(e)
                load_second(e)
            for i in range(2):
                sp.wait_ge(lone_out[i], 16 * (B // 2))
                sp.wait_ge(z_out[i], 16 * NS * (E // 2))

        @block.gpsimd
        def _(pool):
            steps = [0]

            def step(ins):
                steps[0] += 1
                ins.then_inc(pool_step, 1)

            def settle():
                pool.wait_ge(pool_step, steps[0])

            def link(ins):
                step(ins)
                settle()

            step(pool.memset(gray[:, :, :, 0:1], 0.0))
            step(pool.memset(gray[:, :, :, PAD_COLS - 1:PAD_COLS], 0.0))
            step(pool.memset(tap_mask[:, :, :], 0.0))
            pool.memset(zeros[:, :], 0.0).then_inc(pool_const, 1)
            settle()
            for dx in range(TAPS):
                link(pool.affine_select(out=tap_mask[0:TAPS * GR], in_=tap_mask[0:TAPS * GR],
                                        compare_op=ALU.not_equal, fill=1.0, base=-dx * GR,
                                        pattern=[[-1, TAPS], [-1, GO]], channel_multiplier=1))
            link(pool.memset(blank[:, :], 0.0))
            pool.memset(blank[:, D + 1:D + 2].bitcast(U32), NOWHERE).then_inc(pool_const, 1)
            link(pool.memset(ident[:, :], 0.0))
            pool.affine_select(out=ident[:, :], in_=ident[:, :], compare_op=ALU.not_equal, fill=1.0,
                               base=0, pattern=[[-1, P]], channel_multiplier=1).then_inc(pool_const, 1)
            step(pool.memset(causal[:, :], 0.0))
            step(pool.memset(tri[:, :], 1.0))
            step(pool.memset(ones[:, :], 1.0))
            step(pool.memset(onehots[:, 0, :], 0.0))
            step(pool.memset(ymv[:, :, :], 1.0))
            settle()
            step(pool.affine_select(out=causal[:, S - P:S], in_=causal[:, S - P:S], compare_op=ALU.is_ge,
                                    fill=MASKED, base=0, pattern=[[-1, P]], channel_multiplier=1))
            step(pool.affine_select(out=tri[:, :], in_=tri[:, :], compare_op=ALU.is_ge, fill=0.0,
                                    base=0, pattern=[[1, P]], channel_multiplier=-1))
            step(pool.iota(rank[:, :, :], pattern=[[0, SC], [-1, E]], base=E, channel_multiplier=0,
                           allow_small_or_imprecise_dtypes=True))
            step(pool.iota(token_id[:, :], pattern=[[P, T // P]], base=0, channel_multiplier=1))
            settle()
            pool.memset(minus_half[:, 0:4], -0.5).then_inc(pool_const, 1)

            def tokens(b):
                pool.wait_ge(edges_ready, DC * (b + 1))
                if b >= 2:
                    pool.wait_ge(scores_done, b - 1)
                pool.tensor_tensor(xT[:, b % 2], edges_abs[:, :, 0, :], edges_abs[:, :, 1, :], ALU.add
                                   ).then_inc(xT_ready, 1)

            def scale_rows(b):
                pool.wait_ge(var_ready, b + 1)
                if b >= 2:
                    pool.wait_ge(t_ready, SC * (b - 1))
                link(pool.tensor_tensor(rstd[:, b % 2], ve[:, :], minus_half[:, 0:SC], ALU.pow))
                pool.tensor_tensor(nmr[:, b % 2], nmean[:, :], rstd[:, b % 2], ALU.mult).then_inc(rstd_ready, 1)

            def number_rows(b):
                if b >= TR:
                    pool.wait_ge(rows_out[b % TR], 16 * SC * (b // TR))
                step(pool.tensor_copy(trow[:, b % TR, :, D + 1:D + 2].bitcast(U32),
                                      token_id[:, SC * b:SC * b + SC].unsqueeze(2)))

            def scale_lone(b):
                link(pool.tensor_tensor(v2[:, :], rstd[:, b % 2], rstd[:, b % 2], ALU.mult))
                link(pool.tensor_tensor(v2n[:, :], v2[:, :], mv[:, :, 1], ALU.mult))
                link(pool.tensor_scalar(v2e[:, :], v2n[:, :], 1.0, EPS / 4, ALU.mult, ALU.add))
                if b >= 2:
                    pool.wait_ge(lone_ready, b - 1)
                pool.tensor_tensor(lone_scale[:, b % 2], v2e[:, :], minus_half[:, 0:SC], ALU.pow
                                   ).then_inc(lone_scale_ready, 1)

            def exp_bias(b):
                pool.wait_ge(nmax_ready, SC * (b + 1))
                pool.wait_ge(rowc_ready, b + 1)
                if b >= 1:
                    pool.wait_ge(probs_ready, b)
                link(pool.tensor_tensor(nfull[:, :], nmax[:, :], rowc[:, :], ALU.subtract))
                pool.tensor_tensor(nbias[:, :], nfull[:, :], rowc[:, :], ALU.add).then_inc(nbias_ready, 1)

            def scatter(b):
                pool.wait_ge(slot_ready, b + 1)
                pool.wait_ge(factor_ready, b + 1)
                settle()
                if b == 0:
                    pool.wait_ge(blanked, 16 * BLANKS)
                for s in range(SC):
                    pool.indirect_dma_start(
                        dispatched, bass.IndirectOffsetOnAxis(ap=slot[:, b % TR, s:s + 1], axis=0),
                        trow[:, b % TR, s, :], None, bounds_check=E * CAP - 1, oob_is_err=False
                    ).then_inc(rows_out[b % TR], 16)

            def split_low(n):
                e, k = divmod(n, 4)
                c = slice(k * PIECE, (k + 1) * PIECE)
                pool.wait_ge(w_hi_ready, n + 1)
                pool.tensor_tensor(w_lo[:, e % 2, c], w_raw[:, e % 2, c], w_hi[:, e % 2, c].bitcast(F32),
                                   ALU.subtract).then_inc(w_lo_ready, 1)

            tokens(0)
            for i in range(B + 2):
                if 1 <= i <= B:
                    number_rows(i - 1)
                    scale_rows(i - 1)
                if i < B:
                    exp_bias(i)
                if 1 <= i <= B:
                    scale_lone(i - 1)
                if i >= 2:
                    scatter(i - 2)
                if i == 0:
                    tokens(1)
                if i + AHEAD_CONV < B:
                    tokens(i + AHEAD_CONV)
                if 0 <= i - SPLIT_AT < 4:
                    split_low(i - SPLIT_AT)

            def scatter_out(e):
                pool.wait_ge(yvar_ready, e + 1)
                if e >= 2:
                    pool.wait_ge(z_ready, e - 1)
                link(pool.tensor_tensor(yrstd[:, e % 2], yve[:, :], minus_half[:, 0:NS], ALU.pow))
                pool.tensor_tensor(ynmr[:, e % 2], ynmean[:, :], yrstd[:, e % 2], ALU.mult).then_inc(yrstd_ready, 1)
                if e == 0:
                    for i in range(2):
                        pool.wait_ge(lone_out[i], 16 * (B // 2))
                pool.wait_ge(z_ready, e + 1)
                for j, (_, n) in enumerate(SLOTS):
                    pool.indirect_dma_start(
                        out_rows,
                        bass.IndirectOffsetOnAxis(ap=ein[0:n, e, j, D + 1:D + 2].bitcast(U32), axis=0),
                        z[0:n, e % 2, j, :], None, bounds_check=T - 1, oob_is_err=False
                    ).then_inc(z_out[e % 2], 16)

            for e in range(E - 1):
                scatter_out(e)

            pool.wait_ge(z_ready, E - 2)
            e = E - 1

            def send(j):
                n = SLOTS[j][1]
                pool.wait_ge(z_ready, E + j)
                pool.indirect_dma_start(
                    out_rows, bass.IndirectOffsetOnAxis(ap=ein[0:n, e, j, D + 1:D + 2].bitcast(U32), axis=0),
                    z[0:n, e % 2, j, :], None, bounds_check=T - 1, oob_is_err=False
                ).then_inc(z_out[e % 2], 16)

            for j in range(NS):
                pool.wait_ge(yvar_ready, E + j)
                link(pool.tensor_tensor(yrstd[:, e % 2, j:j + 1], yve[:, j:j + 1], minus_half[:, 0:1], ALU.pow))
                pool.tensor_tensor(ynmr[:, e % 2, j:j + 1], ynmean[:, j:j + 1], yrstd[:, e % 2, j:j + 1],
                                   ALU.mult).then_inc(yrstd_ready, 1)
                if j >= 1:
                    send(j - 1)
            send(NS - 1)

        @block.scalar
        def _(act):
            def scale_red(b):
                act.wait_ge(pix_in[b % 2], 16 * (b // 2 + 1))
                if b >= 2:
                    act.wait_ge(gray_ready, b - 1)
                act.activation(red[:, b % 2], pix[:, b % 2, 0], ACT.Copy, scale=GRAY[0]).then_inc(red_ready, 1)

            def edges(b):
                if b >= 1:
                    act.wait_ge(xT_ready, b)
                for c in range(DC):
                    act.wait_ge(conv_done, DC * b + c + 1)
                    act.activation(edges_abs[:, c].rearrange("p f s -> p (f s)"), bank[c][:, :], ACT.Abs
                                   ).then_inc(edges_ready, 1)

            def project_keys(b):
                act.wait_ge(y_done, b + 1)
                if b >= 1:
                    act.wait_ge(scores_done, b)
                for c in range(DC):
                    ins = act.activation(yT[:, c, :], bank[3][:, c * S:(c + 1) * S], ACT.Identity,
                                         bias=key_bias[:, c:c + 1])
                ins.then_inc(yT_ready, 1)

            def project_values(b):
                act.wait_ge(v_done, b + 1)
                if b >= 2:
                    act.wait_ge(attn_done, b - 1)
                act.activation(val[:, b % 2, 0, :], bank[3][:, 0:D], ACT.Copy)
                act.activation(val[:, b % 2, 1, :], bank[4][:, VALUES:VALUES + D], ACT.Copy)

            def row_constant(b):
                if b >= 1:
                    act.wait_ge(nbias_ready, b)
                for s, (at, o) in enumerate(((3, D), (4, VALUES + D))):
                    ins = act.activation(rowc[:, s:s + 1], bank[at][:, o:o + 1], ACT.Identity,
                                         bias=bias_dot[:, 0:1], scale=SCALE)
                ins.then_inc(rowc_ready, 1)

            def probs(b):
                act.wait_ge(nbias_ready, b + 1)
                if b >= 1:
                    act.wait_ge(pT_done, b)
                for s in range(SC):
                    n = (s + 1) * P
                    ins = act.activation(prob[:, s, 0:n], score[:, s, 0:n], ACT.Exp, bias=nbias[:, s:s + 1],
                                         scale=-1.0, accum_out=psumr[:, b % 2, s:s + 1])
                ins.then_inc(probs_ready, 1)

            def prob_t(b):
                act.wait_ge(pT_done, b + 1)
                if b >= 1:
                    act.wait_ge(attn_done, b)
                act.activation(probT[:, :], bank[7][:, 0:S + P], ACT.Copy).then_inc(probT_ready, 1)

            def norm_rows(b):
                act.wait_ge(rstd_ready, b + 1)
                if b >= TR:
                    act.wait_ge(rows_out[b % TR], 16 * SC * (b // TR))
                    act.wait_ge(tT_done, b - TR + 1)
                for s in range(SC):
                    act.activation(trow[:, b % TR, s, 0:D], resid[:, b % 2, s, :], ACT.Identity,
                                   bias=nmr[:, b % 2, s:s + 1], scale=rstd[:, b % 2, s:s + 1]).then_inc(t_ready, 1)

            def norm_lone(b):
                act.wait_ge(lone_scale_ready, b + 1)
                act.wait_ge(t_ready, SC * (b + 1))
                if b >= 2:
                    act.wait_ge(lone_out[b % 2], 16 * (b // 2))
                for s in range(SC):
                    ins = act.activation(lone[:, b % 2, s, :], trow[:, b % TR, s, 0:D], ACT.Copy,
                                         scale=lone_scale[:, b % 2, s:s + 1])
                ins.then_inc(lone_ready, 1)

            def t_t(b):
                act.wait_ge(tT_done, b + 1)
                if b >= 1:
                    act.wait_ge(logits_done, b)
                act.activation(tT[:, :, :].rearrange("p c s -> p (c s)"), bank[2][:, :], ACT.Copy
                               ).then_inc(tT_ready, 1)

            def route_exp(b):
                act.wait_ge(lsub_ready, b + 1)
                act.activation(lexp[:, :, :], lsub[:, :, :], ACT.Exp).then_inc(lexp_ready, 1)

            def split_high(n):
                e, k = divmod(n, 4)
                c = slice(k * PIECE, (k + 1) * PIECE)
                act.wait_ge(w_in[e % 2], 32 * (e // 2 + 1))
                if e >= 2:
                    act.wait_ge(h_used, FC * (e - 1))
                act.activation(w_hi[:, e % 2, c], w_raw[:, e % 2, c], ACT.Copy).then_inc(w_hi_ready, 1)

            scale_red(0)
            act.wait_ge(setup_mm, 1)
            for c in range(DC):
                ins = act.activation(wvT[:, c, 0:D], bank[2][:, c * D:(c + 1) * D], ACT.Copy)
            ins.then_inc(setup_ev, 1)
            scale_red(1)
            edges(0)
            scale_red(2)
            scale_red(3)
            act.wait_ge(setup_ev, 3)
            for i in range(B + 2):
                if 2 <= i:
                    t_t(i - 2)
                if 1 <= i <= B:
                    prob_t(i - 1)
                if i < B:
                    project_keys(i)
                if 2 <= i:
                    norm_lone(i - 2)
                    route_exp(i - 2)
                if 0 <= i - SPLIT_AT < 4:
                    split_high(i - SPLIT_AT)
                if i < B:
                    if i + AHEAD_GRAY < B:
                        scale_red(i + AHEAD_GRAY)
                    project_values(i)
                    row_constant(i)
                if 1 <= i <= B:
                    norm_rows(i - 1)
                if i < B:
                    probs(i)
                if i == 0:
                    edges(1)
                if i + AHEAD_CONV < B:
                    edges(i + AHEAD_CONV)

            def ein_t(e):
                act.wait_ge(einT_done, e + 1)
                if e >= 2:
                    act.wait_ge(h_done, FC * (e - 1))
                for c, b in enumerate((3, 7)):
                    act.activation(einT_hi[:, e % 2, c, :], bank[b][:, 0:CAP], ACT.Copy).then_inc(einT_hi_ready, 1)

            def hidden(e, j):
                n = FC * e + j
                act.wait_ge(h_done, n + 1)
                if n >= 3:
                    act.wait_ge(h_used, n - 2)
                act.activation(h_hi[:, n % 3, :], bank[n % 3][:, 0:CAP], ACT.Relu).then_inc(h_hi_ready, 1)

            def norm_out(e):
                act.wait_ge(yrstd_ready, e + 1)
                if e >= 2:
                    act.wait_ge(z_out[e % 2], 16 * NS * (e // 2))
                for j, (_, n) in enumerate(SLOTS):
                    ins = act.activation(z[0:n, e % 2, j, :], y[0:n, e % 2, j, :], ACT.Identity,
                                         bias=ynmr[0:n, e % 2, j:j + 1], scale=yrstd[0:n, e % 2, j:j + 1])
                ins.then_inc(z_ready, 1)

            ein_t(0)
            for e in range(E):
                for j in range(FC):
                    hidden(e, j)
                    if e >= 2 and j == 1:
                        norm_out(e - 2)
                    if e >= 1 and j == 0:
                        split_high(4 * e + 3)
                    if e + 1 < E:
                        if j in (3, 4, 7):
                            split_high(4 * (e + 1) + (3, 4, 7).index(j))
                        if j == 5:
                            ein_t(e + 1)
            norm_out(E - 2)
            e = E - 1
            act.wait_ge(z_out[e % 2], 16 * NS * (e // 2))
            for j, (_, n) in enumerate(SLOTS):
                act.wait_ge(yrstd_ready, E + j)
                act.activation(z[0:n, e % 2, j, :], y[0:n, e % 2, j, :], ACT.Identity,
                               bias=ynmr[0:n, e % 2, j:j + 1], scale=yrstd[0:n, e % 2, j:j + 1]
                               ).then_inc(z_ready, 1)

        @block.vector
        def _(dve):
            steps = [0]

            def step(ins):
                steps[0] += 1
                ins.then_inc(dve_step, 1)

            def settle():
                dve.wait_ge(dve_step, steps[0])

            def link(ins):
                step(ins)
                settle()

            def make_gray(b):
                dve.wait_ge(red_ready, b + 1)
                if b >= 2:
                    dve.wait_ge(gray_out[b % 2], 16 * (b // 2))
                link(dve.scalar_tensor_tensor(red[:, b % 2], pix[:, b % 2, 1], GRAY[1], red[:, b % 2],
                                              ALU.mult, ALU.add))
                dve.scalar_tensor_tensor(gray[:, b % 2, :, 1:D + 1], pix[:, b % 2, 2], GRAY[2], red[:, b % 2],
                                         ALU.mult, ALU.add).then_inc(gray_ready, 1)

            K = TAPS * GR
            make_gray(0)
            dve.wait_ge(taps_in, 16 * TAPS)
            dve.wait_ge(pool_const, 2)
            link(dve.tensor_scalar(half_taps[0:K], taps[0:K], 0.5, None, ALU.mult))
            for dy in range(TAPS):
                for f in range(2):
                    tap = (f * TAPS + dy) * TAPS
                    w = half_taps[0:K, tap:tap + 1]
                    if dy == 0:
                        ins = dve.tensor_scalar(band[0:K, f, :], tap_mask[0:K, dy, :], w, None, ALU.mult)
                    else:
                        ins = dve.scalar_tensor_tensor(band[0:K, f, :], tap_mask[0:K, dy, :], w,
                                                       band[0:K, f, :], ALU.mult, ALU.add)
                    if dy < TAPS - 1:
                        step(ins)
                    else:
                        ins.then_inc(band_ready, 1)
                settle()

            def residual_in(b, s):
                if s == 0:
                    dve.wait_ge(xnat_done, b + 1)
                ins = dve.tensor_tensor(xb[:, b % 2, s, :], bank[2][:, s * D:(s + 1) * D], bvb[:, :], ALU.add)
                step(ins) if s < SC - 1 else ins.then_inc(xb_ready, 1)

            def softmax_max(b):
                dve.wait_ge(scores_done, b + 1)
                if b >= 1:
                    dve.wait_ge(probs_ready, b)
                for s in range(SC):
                    n = (s + 1) * P
                    dve.tensor_tensor_reduce(score[:, s, 0:n], bank[6][:, s * S:s * S + n],
                                             causal[:, S - n:S], -SCALE, -MASKED, ALU.add, ALU.min,
                                             nmax[:, s:s + 1]).then_inc(nmax_ready, 1)

            def softmax_sum(b):
                dve.wait_ge(probs_ready, b + 1)
                step(dve.reciprocal(rinv[:, b % 2, :], psumr[:, b % 2, :]))

            def attend(b):
                dve.wait_ge(attn_done, b + 1)
                settle()
                dve.wait_ge(xb_ready, b + 1)
                if b >= 2:
                    dve.wait_ge(t_ready, SC * (b - 1))
                for s in range(SC):
                    dve.scalar_tensor_tensor(resid[:, b % 2, s, :], bank[5][:, s * D:(s + 1) * D],
                                             rinv[:, b % 2, s:s + 1], xb[:, b % 2, s, :], ALU.mult, ALU.add
                                             ).then_inc(resid_ready, 1)
                for s in range(SC):
                    dve.wait_ge(resid_ready, SC * b + s + 1)
                    step(dve.bn_stats(stats[:, s, :], resid[:, b % 2, s, :]))
                if b >= 1:
                    dve.wait_ge(lone_scale_ready, b)
                settle()
                for s in range(SC):
                    step(dve.bn_aggr(mv[:, s, :], stats[:, s, :]))
                settle()
                step(dve.tensor_scalar(nmean[:, :], mv[:, :, 0], -1.0, None, ALU.mult))
                dve.tensor_scalar(ve[:, :], mv[:, :, 1], EPS, None, ALU.add).then_inc(var_ready, 1)

            def route(b):
                dve.wait_ge(logits_done, b + 1)
                logits = bank[4][:, LOGITS:LOGITS + SC * E].rearrange("p (s e) -> p s e", e=E)
                link(dve.tensor_reduce(lmax[:, :], logits, AX_X, ALU.max))
                peak = lmax[:, :].unsqueeze(2).broadcast_to([P, SC, E])
                step(dve.tensor_tensor(hit[:, :, :], logits, peak, ALU.is_equal))
                dve.tensor_tensor(lsub[:, :, :], logits, peak, ALU.subtract).then_inc(lsub_ready, 1)
                settle()
                link(dve.tensor_tensor(hrank[:, :, :], hit[:, :, :], rank[:, :, :], ALU.mult))
                link(dve.tensor_reduce(best[:, b % 2], hrank[:, :, :], AX_X, ALU.max))
                link(dve.tensor_tensor(onehot[:, b % 2], rank[:, :, :],
                                       best[:, b % 2].unsqueeze(2).broadcast_to([P, SC, E]), ALU.is_equal))
                link(dve.tensor_tensor(onehots[:, b + 1, :], onehots[:, b, :], onehot[:, b % 2, 0, :], ALU.add))
                dve.tensor_tensor(onehots[:, b + 1, :], onehots[:, b + 1, :], onehot[:, b % 2, 1, :], ALU.add
                                  ).then_inc(onehot_ready, 1)
                dve.wait_ge(onehot_ready, b + 1)

            def factor(b):
                dve.wait_ge(lexp_ready, b + 1)
                link(dve.tensor_reduce(lsum[:, :], lexp[:, :, :], AX_X, ALU.add))
                dve.reciprocal(trow[:, b % TR, :, D], lsum[:, :]).then_inc(factor_ready, 1)

            def assign(b):
                dve.wait_ge(count_done, b + 1)
                count = bank[4][:, COUNTS:COUNTS + SC * E].rearrange("p (s e) -> p s e", e=E)
                step(dve.tensor_tensor(mine[:, :, :], onehot[:, b % 2], count, ALU.mult))
                step(dve.tensor_scalar(base[:, :], best[:, b % 2], -float(CAP), float(E * CAP - 1),
                                       ALU.mult, ALU.add))
                settle()
                link(dve.tensor_reduce(place[:, :], mine[:, :, :], AX_X, ALU.add))
                step(dve.tensor_scalar(over[:, :], place[:, :], float(CAP), float(NOWHERE), ALU.is_gt, ALU.mult))
                step(dve.tensor_tensor(basep[:, :], base[:, :], place[:, :], ALU.add))
                settle()
                if b >= TR:
                    dve.wait_ge(rows_out[b % TR], 16 * SC * (b // TR))
                dve.tensor_tensor(slot[:, b % TR, :], basep[:, :], over[:, :], ALU.add).then_inc(slot_ready, 1)

            dve.wait_ge(setup_mm, 2)
            for c in range(DC):
                ins = dve.tensor_copy(wqk[:, c, :], bank[3][:, c * D:(c + 1) * D])
            ins.then_inc(setup_ev, 1)
            step(dve.tensor_copy(key_bias[:, :], bank[4][:, 0:DC]))
            step(dve.tensor_copy(wvT[:, :, D:D + 1], bank[4][:, DC:2 * DC].unsqueeze(2)))
            settle()
            dve.tensor_scalar(bias_dot[:, :], bank[4][:, 2 * DC:2 * DC + 1], SCALE, None, ALU.mult
                              ).then_inc(setup_ev, 1)
            make_gray(1)
            make_gray(2)
            make_gray(3)
            dve.wait_ge(pool_const, 4)
            for i in range(B + 2):
                if i < B:
                    residual_in(i, 0)
                    residual_in(i, 1)
                if i >= 2:
                    route(i - 2)
                if 1 <= i <= B:
                    attend(i - 1)
                if i >= 2:
                    factor(i - 2)
                if i < B:
                    softmax_max(i)
                if i >= 2:
                    assign(i - 2)
                if i + AHEAD_GRAY < B:
                    make_gray(i + AHEAD_GRAY)
                if i < B:
                    softmax_sum(i)

            def split_low(n):
                e, k = divmod(n, 4)
                c = slice(k * PIECE, (k + 1) * PIECE)
                dve.wait_ge(w_hi_ready, n + 1)
                dve.tensor_tensor(w_lo[:, e % 2, c], w_raw[:, e % 2, c], w_hi[:, e % 2, c].bitcast(F32),
                                  ALU.subtract).then_inc(w_lo_ready, 1)

            def ein_t(e):
                for c, b in enumerate((3, 7)):
                    dve.wait_ge(einT_hi_ready, DC * e + c + 1)
                    ins = dve.tensor_tensor(einT_lo[:, e % 2, c, :], bank[b][:, 0:CAP],
                                            einT_hi[:, e % 2, c, :].bitcast(F32), ALU.subtract)
                ins.then_inc(einT_ready, 1)

            def hidden(e, j):
                n = FC * e + j
                dve.wait_ge(h_hi_ready, n + 1)
                dve.scalar_tensor_tensor(h_lo[:, n % 3, :], bank[n % 3][:, 0:CAP], 0.0,
                                         h_hi[:, n % 3, :].bitcast(F32), ALU.max, ALU.subtract
                                         ).then_inc(h_ready, 1)

            def expert_out(e):
                if e >= 2:
                    dve.wait_ge(z_ready, e - 1)
                for j, (_, n) in enumerate(SLOTS):
                    if j < NS - 1:
                        dve.wait_ge(tile_done, (NS - 1) * e + j + 1)
                    else:
                        dve.wait_ge(h_used, FC * (e + 1))
                    dve.scalar_tensor_tensor(y[0:n, e % 2, j, :], bank[4 + j][0:n, 0:D],
                                             ein[0:n, e, j, D:D + 1], ein[0:n, e, j, 0:D],
                                             ALU.mult, ALU.add).then_inc(y_ready, 1)

            def expert_stats(e):
                for j, (_, n) in enumerate(SLOTS):
                    dve.wait_ge(y_ready, NS * e + j + 1)
                    step(dve.bn_stats(ystats[0:n, j, :], y[0:n, e % 2, j, :]))

            def expert_var(e):
                if e >= 1:
                    dve.wait_ge(yrstd_ready, e)
                settle()
                for j, (_, n) in enumerate(SLOTS):
                    step(dve.bn_aggr(ymv[0:n, j, :], ystats[0:n, j, :]))
                settle()
                step(dve.tensor_scalar(ynmean[:, :], ymv[:, :, 0], -1.0, None, ALU.mult))
                settle()
                dve.tensor_scalar(yve[:, :], ymv[:, :, 1], EPS, None, ALU.add).then_inc(yvar_ready, 1)

            ein_t(0)
            for e in range(E):
                for j in range(FC):
                    hidden(e, j)
                    if e >= 1:
                        if j in (0, 2):
                            split_low(4 * e + 2 + j // 2)
                        if j == 1:
                            expert_out(e - 1)
                        if j == 3:
                            expert_stats(e - 1)
                        if j == 7:
                            expert_var(e - 1)
                    if e + 1 < E:
                        if j in (4, 6):
                            split_low(4 * (e + 1) + (j - 4) // 2)
                        if j == 5:
                            ein_t(e + 1)
            dve.wait_ge(yrstd_ready, E - 1)
            dve.wait_ge(z_ready, E - 2)
            e = E - 1
            for j, (_, n) in enumerate(SLOTS):
                dve.wait_ge(tile_done, (NS - 1) * e + j + 1) if j < NS - 1 else dve.wait_ge(h_used, FC * E)
                dve.scalar_tensor_tensor(y[0:n, e % 2, j, :], bank[4 + j][0:n, 0:D],
                                         ein[0:n, e, j, D:D + 1], ein[0:n, e, j, 0:D],
                                         ALU.mult, ALU.add).then_inc(y_ready, 1)
                dve.wait_ge(y_ready, NS * e + j + 1)
                link(dve.bn_stats(ystats[0:n, j, :], y[0:n, e % 2, j, :]))
                link(dve.bn_aggr(ymv[0:n, j, :], ystats[0:n, j, :]))
                step(dve.tensor_scalar(yve[:, j:j + 1], ymv[:, j, 1:2], EPS, None, ALU.add))
                dve.tensor_scalar(ynmean[:, j:j + 1], ymv[:, j, 0:1], -1.0, None, ALU.mult
                                  ).then_inc(yvar_ready, 1)
                settle()

        @block.tensor
        def _(pe):
            def product(to, a, b, first, last):
                (ah, al), (bh, bl) = a, b
                pe.matmul(to, ah, bh, start=first, stop=False)
                pe.matmul(to, ah, bl, start=False, stop=False)
                return pe.matmul(to, al, bh, start=False, stop=last)

            def setup():
                pe.wait_ge(attn_w_in, 16 * 3)
                pe.wait_ge(pool_const, 3)
                for c in range(DC):
                    for k in range(DC):
                        ins = pe.transpose(bank[2][:, c * D + k * P:c * D + (k + 1) * P],
                                           wv[:, k, c * P:(c + 1) * P], ident[:, :])
                ins.then_inc(setup_mm, 1)
                pe.wait_ge(bias_in, 16 * 2)
                for c in range(DC):
                    for k in range(DC):
                        pe.matmul(bank[3][:, c * D:(c + 1) * D], wq[:, k, c * P:(c + 1) * P], wk[:, k, :],
                                  start=(k == 0), stop=(k == DC - 1))
                for c in range(DC):
                    for k in range(DC):
                        pe.matmul(bank[4][:, c:c + 1], wk[:, k, c * P:(c + 1) * P], bqc[:, k:k + 1],
                                  start=(k == 0), stop=(k == DC - 1))
                for c in range(DC):
                    for k in range(DC):
                        pe.matmul(bank[4][:, DC + c:DC + c + 1], wq[:, k, c * P:(c + 1) * P], bkc[:, k:k + 1],
                                  start=(k == 0), stop=(k == DC - 1))
                for k in range(DC):
                    ins = pe.matmul(bank[4][:, 2 * DC:2 * DC + 1], bqc[:, k:k + 1].broadcast_to([P, P]),
                                    bkc[:, k:k + 1], start=(k == 0), stop=(k == DC - 1))
                ins.then_inc(setup_mm, 1)

            def convolve(b):
                pe.wait_ge(shifted_in[b % 2], 16 * TAPS * (b // 2 + 1))
                K = TAPS * GR
                for c in range(DC):
                    if b >= 1:
                        pe.wait_ge(edges_ready, DC * (b - 1) + c + 1)
                    acc = bank[c][:, :].rearrange("p (f s) -> p f s", f=2)
                    for g in range(GROUPS):
                        n = min(GO, S - g * GO)
                        ins = pe.matmul(acc[:, :, g * GO:g * GO + n], shifted[0:K, b % 2, g, c * P:(c + 1) * P],
                                        band[0:K, :, 0:n], start=True, stop=True)
                    ins.then_inc(conv_done, 1)

            def project_keys(b):
                pe.wait_ge(xT_ready, b + 1)
                if b >= 1:
                    pe.wait_ge(rowc_ready, b)
                for c in range(DC):
                    for k in range(DC):
                        ins = pe.matmul(bank[3][:, c * S:(c + 1) * S], wqk[:, k, c * P:(c + 1) * P],
                                        xT[:, b % 2, k, :], start=(k == 0), stop=(k == DC - 1))
                ins.then_inc(y_done, 1)

            def tokens_as_rows(b):
                if b >= 2:
                    pe.wait_ge(tT_ready, b - 1)
                for s in range(SC):
                    for c in range(DC):
                        ins = pe.transpose(bank[2][:, s * D + c * P:s * D + (c + 1) * P],
                                           xT[:, b % 2, c, s * P:(s + 1) * P], ident[:, :])
                ins.then_inc(xnat_done, 1)

            def project_values(b):
                pe.wait_ge(yT_ready, b + 1)
                for s, (at, o) in enumerate(((3, 0), (4, VALUES))):
                    if s == 1 and b >= 2:
                        pe.wait_ge(onehot_ready, b - 1)
                    for k in range(DC):
                        ins = pe.matmul(bank[at][:, o:o + D + 1], xT[:, b % 2, k, s * P:(s + 1) * P],
                                        wvT[:, k, :], start=(k == 0), stop=(k == DC - 1))
                ins.then_inc(v_done, 1)

            def scores(b):
                if b >= 1:
                    pe.wait_ge(nmax_ready, SC * b)
                for s in range(SC):
                    n = (s + 1) * P
                    for k in range(DC):
                        ins = pe.matmul(bank[6][:, s * S:s * S + n], yT[:, k, s * P:(s + 1) * P],
                                        xT[:, b % 2, k, 0:n], start=(k == 0), stop=(k == DC - 1))
                ins.then_inc(scores_done, 1)

            def prob_t(b):
                pe.wait_ge(probs_ready, b + 1)
                pe.transpose(bank[7][:, 0:P], prob[:, 0, 0:P], ident[:, :])
                pe.transpose(bank[7][:, P:2 * P], prob[:, 1, 0:P], ident[:, :])
                pe.transpose(bank[7][:, 2 * P:3 * P], prob[:, 1, P:2 * P], ident[:, :]).then_inc(pT_done, 1)

            def attend(b):
                pe.wait_ge(probT_ready, b + 1)
                if b >= 1:
                    pe.wait_ge(resid_ready, SC * b)
                pe.matmul(bank[5][:, 0:D], probT[:, 0:P], val[:, b % 2, 0, :], start=True, stop=True)
                pe.matmul(bank[5][:, D:2 * D], probT[:, P:2 * P], val[:, b % 2, 0, :], start=True, stop=False)
                pe.matmul(bank[5][:, D:2 * D], probT[:, 2 * P:3 * P], val[:, b % 2, 1, :], start=False, stop=True
                          ).then_inc(attn_done, 1)

            def turn(b):
                pe.wait_ge(t_ready, SC * (b + 1))
                pe.wait_ge(xb_ready, min(b + 2, B))
                for c in range(DC):
                    for s in range(SC):
                        ins = pe.transpose(bank[2][:, c * S + s * P:c * S + (s + 1) * P],
                                           trow[:, b % TR, s, c * P:(c + 1) * P], ident[:, :])
                ins.then_inc(tT_done, 1)

            def logits(b):
                pe.wait_ge(tT_ready, b + 1)
                if b >= 1:
                    pe.wait_ge(slot_ready, b)
                    pe.wait_ge(rowc_ready, min(b + 2, B))
                for s in range(SC):
                    for k in range(DC):
                        o = LOGITS + s * E
                        ins = pe.matmul(bank[4][:, o:o + E], tT[:, k, s * P:(s + 1) * P], wr[:, k, :],
                                        start=(k == 0), stop=(k == DC - 1))
                ins.then_inc(logits_done, 1)

            def count(b):
                pe.wait_ge(onehot_ready, b + 1)
                pe.wait_ge(rowc_ready, min(b + 3, B))
                o = COUNTS
                pe.matmul(bank[4][:, o:o + E], ones[:, :], onehots[:, b, :], start=True, stop=False)
                pe.matmul(bank[4][:, o:o + E], tri[:, :], onehot[:, b % 2, 0, :], start=False, stop=True)
                pe.matmul(bank[4][:, o + E:o + 2 * E], ones[:, :], onehots[:, b, :], start=True, stop=False)
                pe.matmul(bank[4][:, o + E:o + 2 * E], ones[:, :], onehot[:, b % 2, 0, :], start=False, stop=False)
                pe.matmul(bank[4][:, o + E:o + 2 * E], tri[:, :], onehot[:, b % 2, 1, :], start=False, stop=True
                          ).then_inc(count_done, 1)

            setup()
            pe.wait_ge(band_ready, 2)
            convolve(0)
            pe.wait_ge(setup_ev, 3)
            for i in range(B + 2):
                if 1 <= i <= B:
                    prob_t(i - 1)
                if i < B:
                    project_keys(i)
                    tokens_as_rows(i)
                if 2 <= i:
                    logits(i - 2)
                if 1 <= i <= B:
                    attend(i - 1)
                if i < B:
                    project_values(i)
                    scores(i)
                if i >= 2:
                    count(i - 2)
                if i == 0:
                    convolve(1)
                if i + AHEAD_CONV < B:
                    convolve(i + AHEAD_CONV)
                if 1 <= i <= B:
                    turn(i - 1)

            def ein_t(e):
                pe.wait_ge(ein_in[e], 32)
                if e >= 1:
                    pe.wait_ge(einT_ready, e)
                for c, b in enumerate((3, 7)):
                    for j, (o, n) in enumerate(SLOTS):
                        ins = pe.transpose(bank[b][:, o:o + n], ein[0:n, e, j, c * P:(c + 1) * P],
                                           ident[0:n, 0:n])
                ins.then_inc(einT_done, 1)

            def hidden(e, j):
                n = FC * e + j
                if j == 0:
                    pe.wait_ge(einT_ready, e + 1)
                    pe.wait_ge(w_lo_ready, 4 * e + 2)
                if n >= 3:
                    pe.wait_ge(h_ready, n - 2)
                for k in range(DC):
                    w = slice(k * F + j * P, k * F + (j + 1) * P)
                    ins = product(bank[n % 3][:, 0:CAP], (w_hi[:, e % 2, w], w_lo[:, e % 2, w]),
                                  (einT_hi[:, e % 2, k, :], einT_lo[:, e % 2, k, :]), k == 0, k == DC - 1)
                ins.then_inc(h_done, 1)

            def expert_out(e, j):
                n = FC * e + j
                pe.wait_ge(h_ready, n + 1)
                if j % 4 == 0:
                    pe.wait_ge(w_lo_ready, 4 * e + 3 + j // 4)
                w = slice(DC * F + j * D, DC * F + (j + 1) * D)
                for i, (o, m) in enumerate(SLOTS):
                    if j == 0 and e >= 1:
                        pe.wait_ge(y_ready, NS * (e - 1) + i + 1)
                    ins = product(bank[4 + i][0:m, 0:D], (h_hi[:, n % 3, o:o + m], h_lo[:, n % 3, o:o + m]),
                                  (w_hi[:, e % 2, w], w_lo[:, e % 2, w]), j == 0, j == FC - 1)
                    if j == FC - 1 and i < NS - 1:
                        ins.then_inc(tile_done, 1)
                ins.then_inc(h_used, 1)

            ein_t(0)
            for e in range(E):
                for j in range(FC):
                    hidden(e, j)
                    if j == 5 and e + 1 < E:
                        ein_t(e + 1)
                    n = FC * e + j - 2
                    if n >= 0:
                        expert_out(n // FC, n % FC)
            for j in range(FC - 2, FC):
                expert_out(E - 1, j)


_INS = ['x', 'L0_tok_scharr', 'L0_attn_Wq', 'L0_attn_bq', 'L0_attn_Wk', 'L0_attn_bk', 'L0_attn_Wv', 'L0_attn_bv',
        'L0_ffn_Wr', 'L0_ffn_W1', 'L0_ffn_W2']
_OUTS = [((8, 256, 256), 'float32')]


def kernel(**inputs):
    import numpy as _np
    import concourse.bacc as _bacc
    from concourse import mybir as _mybir
    from concourse.bass_utils import run_bass_kernel_spmd as _run

    nc = _bacc.Bacc("TRN2", target_bir_lowering=False, num_devices=1)
    arrays, args = {}, []
    for name in _INS:
        a = _np.ascontiguousarray(inputs[name])
        arrays[f"in_{name}_dram"] = a
        args.append(nc.dram_tensor(f"in_{name}_dram", a.shape, _mybir.dt.from_np(a.dtype), kind="ExternalInput").ap())
    for i, (shape, dtype) in enumerate(_OUTS):
        dt = _mybir.dt.from_np(_np.dtype(dtype))
        args.append(nc.dram_tensor(f"out_{i}_dram", shape, dt, kind="ExternalOutput").ap())
    vit_tower_kernel(nc, *args)
    r = _run(nc, [arrays], core_ids=[0])
    got = tuple(r.results[0][f"out_{i}_dram"] for i in range(len(_OUTS)))
    return got[0]
```

```python
from contextlib import ExitStack

import numpy as np
import concourse.bass as bass
from concourse import mybir

P = 128
ALU = mybir.AluOpType
ACT = mybir.ActivationFunctionType
AX_X = mybir.AxisListType.X
F32 = mybir.dt.float32
F32R = mybir.dt.float32r
BF16 = mybir.dt.bfloat16
U32 = mybir.dt.uint32

GRAY = (0.2989, 0.587, 0.114)
EPS = 1e-5
MASKED = -3.0e38
CAP_FACTOR = 1.25
NOWHERE = 1 << 20




def vit_tower_kernel(
    nc: bass.Bass,
    x: bass.AP,
    scharr: bass.AP,
    Wq: bass.AP,
    bq: bass.AP,
    Wk: bass.AP,
    bk: bass.AP,
    Wv: bass.AP,
    bv: bass.AP,
    Wr: bass.AP,
    W1: bass.AP,
    W2: bass.AP,
    out: bass.AP,
):
    B, CH, S, D = x.shape
    E, _, F = W1.shape
    DC, SC, FC = D // P, S // P, F // P
    T = B * S
    CAP = int(CAP_FACTOR * T / E)
    TAPS = 3
    GR = P // TAPS
    GO = GR - TAPS + 1
    GROUPS = -(-S // GO)
    HALF_GROUPS = (P + 1 - GR) // GO + 1
    PAD_ROWS = (GROUPS - 1) * GO + GR
    PAD_COLS = D + TAPS - 1
    ROW = D + 2
    SLOTS = [(i, min(P, CAP - i)) for i in range(0, CAP, P)]
    NS = len(SLOTS)
    SCALE = float(D) ** -0.5
    assert D == 2 * P and S == 2 * P and CH == 3 and F % P == 0

    dispatched = nc.dram_tensor("dispatched", [E * CAP, ROW], F32, kind="Internal").ap()
    padded = nc.dram_tensor("padded", [B, PAD_ROWS, PAD_COLS], F32, kind="Internal").ap()
    out_rows = out.rearrange("b s d -> (b s) d")

    with ExitStack() as ctx:
        def sb(name, shape, dt=F32):
            return ctx.enter_context(nc.sbuf_tensor(name, shape, dt))

        def sem(name):
            return ctx.enter_context(nc.semaphore(name))

        bank = [ctx.enter_context(nc.psum_tensor(f"bank{i}", [P, 512], F32)) for i in range(8)]
        LOGITS, COUNTS, VALUES = 0, SC * E, P

        ident = sb("ident", [P, P])
        causal = sb("causal", [P, S])
        tri = sb("tri", [P, P], BF16)
        ones = sb("ones", [P, P], BF16)
        tap_mask = sb("tap_mask", [P, TAPS, GO])
        TAP_COLS = 2 * TAPS * TAPS - (TAPS - 1)
        taps = sb("taps", [P, TAP_COLS])
        half_taps = sb("half_taps", [P, TAP_COLS])
        band = sb("band", [P, 2, GO])
        rank = sb("rank", [P, SC, E])
        token_id = sb("token_id", [P, T // P], U32)
        minus_half = sb("minus_half", [P, 4])
        zeros = sb("zeros", [32, PAD_COLS])
        blank = sb("blank", [P, ROW])
        wq = sb("wq", [P, DC, D])
        wk = sb("wk", [P, DC, D])
        wv = sb("wv", [P, DC, D])
        bqc = sb("bqc", [P, DC])
        bkc = sb("bkc", [P, DC])
        bvb = sb("bvb", [P, D])
        wr = sb("wr", [P, DC, E])
        key_bias = sb("key_bias", [P, DC])
        bias_dot = sb("bias_dot", [P, 1])
        WCOLS = DC * F + FC * D
        PIECE = WCOLS // 4
        w_raw = sb("w_raw", [P, 2, WCOLS])
        w_hi = sb("w_hi", [P, 2, WCOLS], F32R)
        w_lo = sb("w_lo", [P, 2, WCOLS], F32R)
        VCOLS = D + 2
        attn_hi = w_hi[:, 1, :]
        attn_lo = w_lo[:, 1, :]

        def halves(start, *dims):
            n = int(np.prod(dims))
            names = "abc"[:len(dims)]
            cut = f"p ({' '.join(names)}) -> p {' '.join(names)}"
            sizes = dict(zip(names, dims))
            return [t[:, start:start + n].rearrange(cut, **sizes) for t in (attn_hi, attn_lo)]

        xT_hi, xT_lo = halves(0, 2, DC, S)
        yT_hi, yT_lo = halves(2 * DC * S, DC, S)
        wqk_hi, wqk_lo = halves(3 * DC * S, DC, D)
        wvT_hi, wvT_lo = halves(3 * DC * S + DC * D, DC, VCOLS)
        assert 3 * DC * S + DC * (D + VCOLS) <= WCOLS
        PIX, SHIFTED, EIN = 2 * CH * SC * D, 2 * GROUPS * D, E * NS * ROW
        images = sb("images", [P, max(PIX + SHIFTED, EIN)])
        pix = images[:, 0:PIX].rearrange("p (b c s d) -> p b c s d", b=2, c=CH, s=SC)
        red = sb("red", [P, 2, SC, D])
        gray = sb("gray", [P, 2, SC, PAD_COLS])
        shifted = images[0:TAPS * GR, PIX:PIX + SHIFTED].rearrange("p (b g d) -> p b g d", b=2, g=GROUPS)
        tokens_mem = sb("tokens_mem", [P, max(12 * D, 4 * NS * D)])
        edges_abs = tokens_mem[:, 0:4 * D].rearrange("p (c f s) -> p c f s", c=DC, f=2)
        xT = sb("xT", [P, 2, DC, S])
        xb = tokens_mem[:, 4 * D:8 * D].rearrange("p (b s d) -> p b s d", b=2, s=SC)
        val = sb("val", [P, 2, SC, D])
        score = tokens_mem[:, 10 * D:12 * D].rearrange("p (c s) -> p c s", c=SC)
        nmax = sb("nmax", [P, SC])
        rowc = sb("rowc", [P, SC])
        nfull = sb("nfull", [P, SC])
        nbias = sb("nbias", [P, SC])
        prob = sb("prob", [P, SC, S])
        psumr = sb("psumr", [P, 2, SC])
        rinv = sb("rinv", [P, 2, SC])
        probT = sb("probT", [P, S + P])
        resid = sb("resid", [P, 2, SC, D])
        stats = sb("stats", [P, SC, 6])
        mv = sb("mv", [P, SC, 2])
        ve = sb("ve", [P, SC])
        nmean = sb("nmean", [P, SC])
        rstd = sb("rstd", [P, 2, SC])
        nmr = sb("nmr", [P, 2, SC])
        v2 = sb("v2", [P, SC])
        v2n = sb("v2n", [P, SC])
        v2e = sb("v2e", [P, SC])
        lone_scale = sb("lone_scale", [P, 2, SC])
        TR = 3
        trow = sb("trow", [P, TR, SC, ROW])
        tT = sb("tT", [P, DC, S])
        lone = sb("lone", [P, 2, SC, D])
        lmax = sb("lmax", [P, SC])
        hit = sb("hit", [P, SC, E])
        hrank = sb("hrank", [P, SC, E])
        best = sb("best", [P, 2, SC])
        onehot = sb("onehot", [P, 2, SC, E], BF16)
        onehots = sb("onehots", [P, B + 1, E], BF16)
        lsub = sb("lsub", [P, SC, E])
        lexp = sb("lexp", [P, SC, E])
        lsum = sb("lsum", [P, SC])
        mine = sb("mine", [P, SC, E])
        place = sb("place", [P, SC])
        over = sb("over", [P, SC])
        base = sb("base", [P, SC])
        basep = sb("basep", [P, SC])
        slot = sb("slot", [P, TR, SC], U32)
        ein = images[:, 0:EIN].rearrange("p (e j r) -> p e j r", e=E, j=NS)
        einT_hi = sb("einT_hi", [P, 2, DC, CAP], F32R)
        einT_lo = sb("einT_lo", [P, 2, DC, CAP], F32R)
        def hidden_halves(n):
            if n >= FC * (E - 1) + 2:
                c = slice((n % FC) * CAP, (n % FC + 1) * CAP)
                return w_hi[:, E % 2, c], w_lo[:, E % 2, c]
            return h_hi[:, n % 3, :], h_lo[:, n % 3, :]

        h_hi = sb("h_hi", [P, 3, CAP], F32R)
        h_lo = sb("h_lo", [P, 3, CAP], F32R)
        sums = sb("sums", [P, DC, CAP])
        SUM_BANKS, TURNED, LAST_BANKS = (4, 5), ((2, 0), (2, D), (6, 0)), (3, 7, 4)
        y = tokens_mem[:, 0:2 * NS * D].rearrange("p (b j d) -> p b j d", b=2, j=NS)
        ystats = sb("ystats", [P, NS, 6])
        ymv = sb("ymv", [P, NS, 2])
        yve = sb("yve", [P, NS])
        ynmean = sb("ynmean", [P, NS])
        yrstd = sb("yrstd", [P, 2, NS])
        ynmr = sb("ynmr", [P, 2, NS])
        z = tokens_mem[:, 2 * NS * D:4 * NS * D].rearrange("p (b j d) -> p b j d", b=2, j=NS)

        taps_in = sem("taps_in")
        bias_in = sem("bias_in")
        consts_in = sem("consts_in")
        attn_w_in = sem("attn_w_in")
        w_in = [sem(f"w_in{i}") for i in range(2)]
        pix_in = [sem(f"pix_in{i}") for i in range(2)]
        first_pix = sem("first_pix")
        first_red = sem("first_red")
        first_gray = sem("first_gray")
        first_out = sem("first_out")
        first_shifted = sem("first_shifted")
        frame_out = sem("frame_out")
        gray_out = [sem(f"gray_out{i}") for i in range(2)]
        shifted_in = [sem(f"shifted_in{i}") for i in range(2)]
        blanked = sem("blanked")
        rows_out = [sem(f"rows_out{i}") for i in range(TR)]
        lone_out = [sem(f"lone_out{i}") for i in range(2)]
        ein_in = [sem(f"ein_in{i}") for i in range(E)]
        z_out = [sem(f"z_out{i}") for i in range(2)]
        pool_const = sem("pool_const")
        pool_step = sem("pool_step")
        dve_step = sem("dve_step")
        band_ready = sem("band_ready")
        setup_mm = sem("setup_mm")
        setup_ev = sem("setup_ev")
        red_ready = sem("red_ready")
        gray_ready = sem("gray_ready")
        conv_done = sem("conv_done")
        edges_ready = sem("edges_ready")
        xT_ready = sem("xT_ready")
        xnat_done = sem("xnat_done")
        chunk_done = sem("chunk_done")
        sum_ready = sem("sum_ready")
        turned = sem("turned")
        last_done = sem("last_done")
        y_done = sem("y_done")
        v_done = sem("v_done")
        xb_ready = sem("xb_ready")
        xT_hi_ready = sem("xT_hi_ready")
        xT_lo_ready = sem("xT_lo_ready")
        yT_hi_ready = sem("yT_hi_ready")
        yT_ready = sem("yT_ready")
        wv_hi_ready = sem("wv_hi_ready")
        rowc_ready = sem("rowc_ready")
        scores_done = sem("scores_done")
        nmax_ready = sem("nmax_ready")
        nbias_ready = sem("nbias_ready")
        probs_ready = sem("probs_ready")
        pT_done = sem("pT_done")
        probT_ready = sem("probT_ready")
        attn_done = sem("attn_done")
        resid_ready = sem("resid_ready")
        var_ready = sem("var_ready")
        rstd_ready = sem("rstd_ready")
        t_ready = sem("t_ready")
        lone_scale_ready = sem("lone_scale_ready")
        lone_ready = sem("lone_ready")
        tT_done = sem("tT_done")
        tT_ready = sem("tT_ready")
        logits_done = sem("logits_done")
        lsub_ready = sem("lsub_ready")
        lexp_ready = sem("lexp_ready")
        onehot_ready = sem("onehot_ready")
        count_done = sem("count_done")
        slot_ready = sem("slot_ready")
        factor_ready = sem("factor_ready")
        w_hi_ready = sem("w_hi_ready")
        w_lo_ready = sem("w_lo_ready")
        einT_done = sem("einT_done")
        einT_hi_ready = sem("einT_hi_ready")
        einT_ready = sem("einT_ready")
        h_done = sem("h_done")
        h_hi_ready = sem("h_hi_ready")
        h_ready = sem("h_ready")
        h_used = sem("h_used")
        y_ready = sem("y_ready")
        yvar_ready = sem("yvar_ready")
        yrstd_ready = sem("yrstd_ready")
        z_ready = sem("z_ready")

        block = ctx.enter_context(nc.Block())

        dispatched_w = dispatched.rearrange("(k p) r -> p k r", p=P)
        BLANKS = 4
        KB = E * CAP // P // BLANKS
        AHEAD_CONV, AHEAD_GRAY = 2, 4
        L = B - 1
        SPLIT_AT, SPLIT_EARLY = 4, 2

        def route_bank(b):
            return bank[4] if b < L - 1 else bank[b - (L - 1)]


        @block.sync
        def _(sp):
            def load_picture(b):
                if b >= 2:
                    sp.wait_ge(gray_ready, b - 1)
                sp.dma_start(pix[:, b % 2].rearrange("p c s d -> p (c s) d"),
                             x[b].rearrange("c (s p) d -> p (c s) d", p=P)).then_inc(pix_in[b % 2], 16)

            def store_gray(b):
                sp.wait_ge(gray_ready, b + 1)
                sp.dma_start(padded[b, 1:1 + S, :].rearrange("(s p) d -> p s d", p=P), gray[:, b % 2]
                             ).then_inc(gray_out[b % 2], 16)

            def load_groups(b, first, end, signal):
                for dx in range(TAPS):
                    src = bass.AP(padded.tensor, padded[b, first * GO, dx].offset,
                                  [[PAD_COLS, GR], [GO * PAD_COLS, end - first], [1, D]])
                    sp.dma_start(shifted[dx * GR:(dx + 1) * GR, b % 2, first:end], src).then_inc(signal, 16)

            def load_shifted(b):
                sp.wait_ge(gray_out[b % 2], 16 * (b // 2 + 1))
                if b >= 2:
                    sp.wait_ge(conv_done, DC * (b - 1))
                load_groups(b, 0, GROUPS, shifted_in[b % 2])

            def load_first(e):
                if e >= 2:
                    sp.wait_ge(w_lo_ready, 4 * (e - 1))
                sp.dma_start(w_raw[:, e % 2, 0:DC * F].rearrange("p (c f) -> p c f", c=DC),
                             W1[e].rearrange("(c p) f -> p c f", p=P)).then_inc(w_in[e % 2], 16)

            def load_second(e):
                sp.dma_start(w_raw[:, e % 2, DC * F:WCOLS].rearrange("p (c d) -> p c d", c=FC),
                             W2[e].rearrange("(c p) d -> p c d", p=P)).then_inc(w_in[e % 2], 16)

            def store_lone(b):
                sp.wait_ge(lone_ready, b + 1)
                sp.dma_start(out_rows[b * S:(b + 1) * S].rearrange("(s p) d -> p s d", p=P), lone[:, b % 2]
                             ).then_inc(lone_out[b % 2], 16)

            def fill_table(k):
                sp.dma_start(dispatched_w[:, k * KB:(k + 1) * KB, :],
                             blank[:, :].unsqueeze(1).broadcast_to([P, KB, ROW])).then_inc(blanked, 16)

            sp.dma_start(pix[:, 0, :, 0, :], x[0, :, 0:P, :].rearrange("c p d -> p c d")).then_inc(first_pix, 16)
            sp.dma_start(pix[:, 0, :, 1, :], x[0, :, P:S, :].rearrange("c p d -> p c d")).then_inc(pix_in[0], 16)
            for dx in range(TAPS):
                src = bass.AP(scharr.tensor, dx, [[0, GR], [1, TAP_COLS]])
                sp.dma_start(taps[dx * GR:(dx + 1) * GR], src).then_inc(taps_in, 16)
            sp.wait_ge(pool_const, 1)
            sp.dma_start(padded[:, 0, :], zeros[0:B, :]).then_inc(frame_out, 16)
            sp.dma_start(padded[:, 1 + S:PAD_ROWS, :].rearrange("b r c -> r b c"),
                         zeros[0:PAD_ROWS - 1 - S, :].unsqueeze(1).broadcast_to(
                             [PAD_ROWS - 1 - S, B, PAD_COLS])).then_inc(frame_out, 16)
            sp.dma_start(wv[:, :, :], Wv.rearrange("(c p) d -> p c d", p=P)).then_inc(attn_w_in, 16)
            sp.dma_start(wq[:, :, :], Wq.rearrange("(p c) d -> p c d", c=DC)).then_inc(attn_w_in, 16)
            sp.dma_start(wk[:, :, :], Wk.rearrange("(p c) d -> p c d", c=DC)).then_inc(attn_w_in, 16)
            sp.wait_ge(first_gray, 1)
            sp.dma_start(padded[0, 1:1 + P, :], gray[:, 0, 0]).then_inc(first_out, 16)
            sp.wait_ge(gray_ready, 1)
            sp.dma_start(padded[0, 1 + P:1 + S, :], gray[:, 0, 1]).then_inc(gray_out[0], 16)
            sp.dma_start(bqc[:, :], bq.rearrange("(p c) -> p c", c=DC)).then_inc(bias_in, 16)
            sp.dma_start(bkc[:, :], bk.rearrange("(p c) -> p c", c=DC)).then_inc(bias_in, 16)
            load_picture(1)
            sp.wait_ge(frame_out, 32)
            sp.wait_ge(first_out, 16)
            load_groups(0, 0, HALF_GROUPS, first_shifted)
            sp.wait_ge(gray_out[0], 16)
            load_groups(0, HALF_GROUPS, GROUPS, shifted_in[0])
            load_picture(2)
            sp.dma_start(bvb[:, :], bv.rearrange("(o d) -> o d", o=1).broadcast_to([P, D])).then_inc(consts_in, 16)
            sp.dma_start(wr[:, :, :], Wr.rearrange("(c p) e -> p c e", p=P)).then_inc(consts_in, 16)
            sp.wait_ge(pool_const, 2)
            for b in range(1, AHEAD_GRAY):
                store_gray(b)
                load_picture(b + 2)
                if b <= AHEAD_CONV:
                    load_shifted(b)
            for i in range(B + 2):
                if i + AHEAD_CONV + 1 < B:
                    load_shifted(i + AHEAD_CONV + 1)
                if i < 2:
                    fill_table(2 * i)
                    fill_table(2 * i + 1)
                elif i < 6:
                    load_first((i - 2) // 2) if i % 2 == 0 else load_second((i - 2) // 2)
                if i >= 2:
                    store_lone(i - 2)
                if i + AHEAD_GRAY < B:
                    store_gray(i + AHEAD_GRAY)
                if i + AHEAD_GRAY + 2 < B:
                    load_picture(i + AHEAD_GRAY + 2)

            for i in range(TR):
                sp.wait_ge(rows_out[i], 16 * SC * len(range(i, B, TR)))
            full = CAP // P
            for e in range(E):
                sp.dma_start(ein[:, e, 0:full, :],
                             dispatched[e * CAP:e * CAP + full * P].rearrange("(j p) r -> p j r", p=P)
                             ).then_inc(ein_in[e], 16)
                sp.dma_start(ein[0:CAP - full * P, e, full, :],
                             dispatched[e * CAP + full * P:(e + 1) * CAP]).then_inc(ein_in[e], 16)
            for e in range(2, E):
                load_first(e)
                load_second(e)
            for i in range(2):
                sp.wait_ge(lone_out[i], 16 * (B // 2))
                sp.wait_ge(z_out[i], 16 * NS * (E // 2))

        @block.gpsimd
        def _(pool):
            steps = [0]

            def step(ins):
                steps[0] += 1
                ins.then_inc(pool_step, 1)

            def settle():
                pool.wait_ge(pool_step, steps[0])

            def link(ins):
                step(ins)
                settle()

            step(pool.memset(gray[:, :, :, 0:1], 0.0))
            step(pool.memset(gray[:, :, :, PAD_COLS - 1:PAD_COLS], 0.0))
            step(pool.memset(tap_mask[:, :, :], 0.0))
            pool.memset(zeros[:, :], 0.0).then_inc(pool_const, 1)
            settle()
            for dx in range(TAPS):
                link(pool.affine_select(out=tap_mask[0:TAPS * GR], in_=tap_mask[0:TAPS * GR],
                                        compare_op=ALU.not_equal, fill=1.0, base=-dx * GR,
                                        pattern=[[-1, TAPS], [-1, GO]], channel_multiplier=1))
            link(pool.memset(blank[:, :], 0.0))
            pool.memset(blank[:, D + 1:D + 2].bitcast(U32), NOWHERE).then_inc(pool_const, 1)
            link(pool.memset(ident[:, :], 0.0))
            pool.affine_select(out=ident[:, :], in_=ident[:, :], compare_op=ALU.not_equal, fill=1.0,
                               base=0, pattern=[[-1, P]], channel_multiplier=1).then_inc(pool_const, 1)
            step(pool.memset(causal[:, :], 0.0))
            step(pool.memset(tri[:, :], 1.0))
            step(pool.memset(ones[:, :], 1.0))
            step(pool.memset(onehots[:, 0, :], 0.0))
            step(pool.memset(ymv[:, :, :], 1.0))
            settle()
            step(pool.affine_select(out=causal[:, S - P:S], in_=causal[:, S - P:S], compare_op=ALU.is_ge,
                                    fill=MASKED, base=0, pattern=[[-1, P]], channel_multiplier=1))
            step(pool.affine_select(out=tri[:, :], in_=tri[:, :], compare_op=ALU.is_ge, fill=0.0,
                                    base=0, pattern=[[1, P]], channel_multiplier=-1))
            step(pool.iota(rank[:, :, :], pattern=[[0, SC], [-1, E]], base=E, channel_multiplier=0,
                           allow_small_or_imprecise_dtypes=True))
            step(pool.iota(token_id[:, :], pattern=[[P, T // P]], base=0, channel_multiplier=1))
            settle()
            pool.memset(minus_half[:, 0:4], -0.5).then_inc(pool_const, 1)

            def tokens(b):
                pool.wait_ge(edges_ready, DC * (b + 1))
                if b >= 2:
                    pool.wait_ge(scores_done, b - 1)
                pool.tensor_tensor(xT[:, b % 2], edges_abs[:, :, 0, :], edges_abs[:, :, 1, :], ALU.add
                                   ).then_inc(xT_ready, 1)

            def tokens_low(b):
                pool.wait_ge(xT_hi_ready, b + 1)
                pool.tensor_tensor(xT_lo[:, b % 2], xT[:, b % 2], xT_hi[:, b % 2].bitcast(F32), ALU.subtract
                                   ).then_inc(xT_lo_ready, 1)

            def scale_rows(b):
                pool.wait_ge(var_ready, b + 1)
                if b >= 2:
                    pool.wait_ge(t_ready, SC * (b - 1))
                link(pool.tensor_tensor(rstd[:, b % 2], ve[:, :], minus_half[:, 0:SC], ALU.pow))
                pool.tensor_tensor(nmr[:, b % 2], nmean[:, :], rstd[:, b % 2], ALU.mult).then_inc(rstd_ready, 1)

            def number_rows(b):
                if b >= TR:
                    pool.wait_ge(rows_out[b % TR], 16 * SC * (b // TR))
                step(pool.tensor_copy(trow[:, b % TR, :, D + 1:D + 2].bitcast(U32),
                                      token_id[:, SC * b:SC * b + SC].unsqueeze(2)))

            def scale_lone(b):
                link(pool.tensor_tensor(v2[:, :], rstd[:, b % 2], rstd[:, b % 2], ALU.mult))
                link(pool.tensor_tensor(v2n[:, :], v2[:, :], mv[:, :, 1], ALU.mult))
                link(pool.tensor_scalar(v2e[:, :], v2n[:, :], 1.0, EPS / 4, ALU.mult, ALU.add))
                if b >= 2:
                    pool.wait_ge(lone_ready, b - 1)
                pool.tensor_tensor(lone_scale[:, b % 2], v2e[:, :], minus_half[:, 0:SC], ALU.pow
                                   ).then_inc(lone_scale_ready, 1)

            def exp_bias(b):
                pool.wait_ge(nmax_ready, SC * (b + 1))
                pool.wait_ge(rowc_ready, b + 1)
                if b >= 1:
                    pool.wait_ge(probs_ready, b)
                link(pool.tensor_tensor(nfull[:, :], nmax[:, :], rowc[:, :], ALU.subtract))
                pool.tensor_tensor(nbias[:, :], nfull[:, :], rowc[:, :], ALU.add).then_inc(nbias_ready, 1)

            def scatter(b):
                pool.wait_ge(slot_ready, b + 1)
                pool.wait_ge(factor_ready, b + 1)
                settle()
                if b == 0:
                    pool.wait_ge(blanked, 16 * BLANKS)
                for s in range(SC):
                    pool.indirect_dma_start(
                        dispatched, bass.IndirectOffsetOnAxis(ap=slot[:, b % TR, s:s + 1], axis=0),
                        trow[:, b % TR, s, :], None, bounds_check=E * CAP - 1, oob_is_err=False
                    ).then_inc(rows_out[b % TR], 16)

            def split_low(n):
                e, k = divmod(n, 4)
                c = slice(k * PIECE, (k + 1) * PIECE)
                pool.wait_ge(w_hi_ready, n + 1)
                pool.tensor_tensor(w_lo[:, e % 2, c], w_raw[:, e % 2, c], w_hi[:, e % 2, c].bitcast(F32),
                                   ALU.subtract).then_inc(w_lo_ready, 1)

            for i in range(L):
                if i >= 1:
                    number_rows(i - 1)
                    tokens_low(i + 1)
                    scale_rows(i - 1)
                exp_bias(i)
                if i >= 1:
                    scale_lone(i - 1)
                if i >= 2:
                    scatter(i - 2)
                if i == 0:
                    tokens(1)
                    tokens_low(1)
                if i + AHEAD_CONV < B:
                    tokens(i + AHEAD_CONV)
                if 0 <= i - SPLIT_AT < SPLIT_EARLY:
                    split_low(i - SPLIT_AT)
            number_rows(L - 1)
            exp_bias(L)
            scale_rows(L - 1)
            scale_lone(L - 1)
            number_rows(L)
            scale_rows(L)
            scale_lone(L)
            scatter(L - 2)
            scatter(L - 1)
            scatter(L)

            def scale_out(e):
                pool.wait_ge(yvar_ready, e + 1)
                if e >= 2:
                    pool.wait_ge(z_ready, e - 1)
                link(pool.tensor_tensor(yrstd[:, e % 2], yve[:, :], minus_half[:, 0:NS], ALU.pow))
                pool.tensor_tensor(ynmr[:, e % 2], ynmean[:, :], yrstd[:, e % 2], ALU.mult).then_inc(yrstd_ready, 1)

            def scatter_tile(e, j):
                n = SLOTS[j][1]
                pool.indirect_dma_start(
                    out_rows, bass.IndirectOffsetOnAxis(ap=ein[0:n, e, j, D + 1:D + 2].bitcast(U32), axis=0),
                    z[0:n, e % 2, j, :], None, bounds_check=T - 1, oob_is_err=False
                ).then_inc(z_out[e % 2], 16)

            def scatter_out(e):
                if e == 0:
                    for i in range(2):
                        pool.wait_ge(lone_out[i], 16 * (B // 2))
                pool.wait_ge(z_ready, e + 1)
                for j in range(NS):
                    scatter_tile(e, j)

            for e in range(E - 1):
                scale_out(e)
                if e < E - 2:
                    scatter_out(e)

            def scale_last(j):
                e, c = E - 1, slice(j, j + 1)
                pool.wait_ge(yvar_ready, E + j)
                link(pool.tensor_tensor(yrstd[:, e % 2, c], yve[:, c], minus_half[:, c], ALU.pow))
                pool.tensor_tensor(ynmr[:, e % 2, c], ynmean[:, c], yrstd[:, e % 2, c], ALU.mult
                                   ).then_inc(yrstd_ready, 1)

            scale_last(0)
            scatter_out(E - 2)
            for j in range(NS):
                if j + 1 < NS:
                    scale_last(j + 1)
                pool.wait_ge(z_ready, E + j)
                scatter_tile(E - 1, j)

        @block.scalar
        def _(act):
            def scale_red(b):
                act.wait_ge(pix_in[b % 2], 16 * (b // 2 + 1))
                if b >= 2:
                    act.wait_ge(gray_ready, b - 1)
                act.activation(red[:, b % 2], pix[:, b % 2, 0], ACT.Copy, scale=GRAY[0]).then_inc(red_ready, 1)

            def edges(b):
                if b >= 1:
                    act.wait_ge(xT_ready, b)
                for c in range(DC):
                    act.wait_ge(conv_done, DC * b + c + 1)
                    act.activation(edges_abs[:, c].rearrange("p f s -> p (f s)"), bank[c][:, :], ACT.Abs
                                   ).then_inc(edges_ready, 1)

            def tokens_high(b):
                act.wait_ge(xT_ready, b + 1)
                if b >= 2:
                    act.wait_ge(scores_done, b - 1)
                act.activation(xT_hi[:, b % 2], xT[:, b % 2], ACT.Copy).then_inc(xT_hi_ready, 1)

            def project_keys(b):
                act.wait_ge(y_done, b + 1)
                if b >= 1:
                    act.wait_ge(scores_done, b)
                for c in range(DC):
                    ins = act.activation(yT_hi[:, c, :], bank[3][:, c * S:(c + 1) * S], ACT.Identity,
                                         bias=key_bias[:, c:c + 1])
                ins.then_inc(yT_hi_ready, 1)

            def project_values(b):
                act.wait_ge(v_done, b + 1)
                if b >= 2:
                    act.wait_ge(attn_done, b - 1)
                act.activation(val[:, b % 2, 0, :], bank[3][:, 0:D], ACT.Copy)
                act.activation(val[:, b % 2, 1, :], bank[4][:, VALUES:VALUES + D], ACT.Copy)

            def row_constant(b):
                if b >= 1:
                    act.wait_ge(nbias_ready, b)
                for s, (at, o) in enumerate(((3, D), (4, VALUES + D))):
                    ins = act.activation(rowc[:, s:s + 1], bank[at][:, o:o + 1], ACT.Identity,
                                         bias=bias_dot[:, 0:1], scale=SCALE)
                ins.then_inc(rowc_ready, 1)

            def probs(b):
                act.wait_ge(nbias_ready, b + 1)
                if b >= 1:
                    act.wait_ge(pT_done, b)
                for s in range(SC):
                    n = (s + 1) * P
                    ins = act.activation(prob[:, s, 0:n], score[:, s, 0:n], ACT.Exp, bias=nbias[:, s:s + 1],
                                         scale=-1.0, accum_out=psumr[:, b % 2, s:s + 1])
                ins.then_inc(probs_ready, 1)

            def prob_t(b):
                act.wait_ge(pT_done, b + 1)
                if b >= 1:
                    act.wait_ge(attn_done, b)
                act.activation(probT[:, :], bank[7][:, 0:S + P], ACT.Copy).then_inc(probT_ready, 1)

            def norm_rows(b):
                act.wait_ge(rstd_ready, b + 1)
                if b >= TR:
                    act.wait_ge(rows_out[b % TR], 16 * SC * (b // TR))
                    act.wait_ge(tT_done, b - TR + 1)
                for s in range(SC):
                    act.activation(trow[:, b % TR, s, 0:D], resid[:, b % 2, s, :], ACT.Identity,
                                   bias=nmr[:, b % 2, s:s + 1], scale=rstd[:, b % 2, s:s + 1]).then_inc(t_ready, 1)

            def norm_lone(b):
                act.wait_ge(lone_scale_ready, b + 1)
                act.wait_ge(t_ready, SC * (b + 1))
                if b >= 2:
                    act.wait_ge(lone_out[b % 2], 16 * (b // 2))
                for s in range(SC):
                    ins = act.activation(lone[:, b % 2, s, :], trow[:, b % TR, s, 0:D], ACT.Copy,
                                         scale=lone_scale[:, b % 2, s:s + 1])
                ins.then_inc(lone_ready, 1)

            def t_t(b):
                act.wait_ge(tT_done, b + 1)
                if b >= 1:
                    act.wait_ge(logits_done, b)
                act.activation(tT[:, :, :].rearrange("p c s -> p (c s)"), bank[2][:, :], ACT.Copy
                               ).then_inc(tT_ready, 1)

            def route_exp(b):
                act.wait_ge(lsub_ready, b + 1)
                act.activation(lexp[:, :, :], lsub[:, :, :], ACT.Exp).then_inc(lexp_ready, 1)

            def split_high(n):
                e, k = divmod(n, 4)
                c = slice(k * PIECE, (k + 1) * PIECE)
                act.wait_ge(w_in[e % 2], 32 * (e // 2 + 1))
                if e >= 2:
                    act.wait_ge(h_used, FC * (e - 1))
                act.activation(w_hi[:, e % 2, c], w_raw[:, e % 2, c], ACT.Copy).then_inc(w_hi_ready, 1)

            act.wait_ge(first_pix, 16)
            act.activation(red[:, 0, 0], pix[:, 0, 0, 0], ACT.Copy, scale=GRAY[0]).then_inc(first_red, 1)
            act.wait_ge(pix_in[0], 16)
            act.activation(red[:, 0, 1], pix[:, 0, 0, 1], ACT.Copy, scale=GRAY[0]).then_inc(red_ready, 1)
            act.wait_ge(setup_mm, 1)
            for c in range(DC):
                ins = act.activation(wvT_hi[:, c, 0:D], bank[2][:, c * D:(c + 1) * D], ACT.Copy)
            ins.then_inc(wv_hi_ready, 1)
            scale_red(1)
            edges(0)
            tokens_high(0)
            scale_red(2)
            act.wait_ge(setup_ev, 2)
            for i in range(L):
                if i >= 2:
                    t_t(i - 2)
                if i >= 1:
                    prob_t(i - 1)
                project_keys(i)
                if i >= 1:
                    tokens_high(i + 1)
                if i >= 2:
                    norm_lone(i - 2)
                    route_exp(i - 2)
                if 0 <= i - SPLIT_AT < SPLIT_EARLY:
                    split_high(i - SPLIT_AT)
                if i == 0:
                    scale_red(AHEAD_GRAY - 1)
                elif i + AHEAD_GRAY < B:
                    scale_red(i + AHEAD_GRAY)
                project_values(i)
                row_constant(i)
                if i >= 1:
                    norm_rows(i - 1)
                if i == L - 1:
                    project_keys(L)
                probs(i)
                if i == 0:
                    edges(1)
                    scale_red(AHEAD_GRAY)
                    tokens_high(1)
                if i + AHEAD_CONV < B:
                    edges(i + AHEAD_CONV)
            t_t(L - 2)
            project_values(L)
            row_constant(L)
            prob_t(L - 1)
            probs(L)
            prob_t(L)
            norm_lone(L - 2)
            norm_rows(L - 1)
            t_t(L - 1)
            route_exp(L - 2)
            norm_rows(L)
            route_exp(L - 1)
            t_t(L)
            norm_lone(L - 1)
            route_exp(L)
            norm_lone(L)
            for n in range(SPLIT_EARLY, 4):
                split_high(n)

            def ein_t(e):
                if e >= 2:
                    act.wait_ge(h_done, FC * (e - 1))
                for c, b in enumerate((3, 7)):
                    act.wait_ge(einT_done, DC * e + c + 1)
                    act.activation(einT_hi[:, e % 2, c, :], bank[b][:, 0:CAP], ACT.Copy).then_inc(einT_hi_ready, 1)

            def hidden(e, j):
                n = FC * e + j
                act.wait_ge(h_done, n + 1)
                if n >= 3:
                    act.wait_ge(h_used, min(n - 2, FC * (E - 1)))
                act.activation(hidden_halves(n)[0], bank[n % 2][:, 0:CAP], ACT.Relu).then_inc(h_hi_ready, 1)

            def store_sums(e):
                if e >= 1:
                    act.wait_ge(turned, e)
                for c in range(DC):
                    if c < DC - 1:
                        act.wait_ge(chunk_done, (DC - 1) * e + c + 1)
                    else:
                        act.wait_ge(h_used, FC * (e + 1))
                    act.activation(sums[:, c, :], bank[SUM_BANKS[c]][:, 0:CAP], ACT.Copy).then_inc(sum_ready, 1)

            def norm_out(e):
                act.wait_ge(yrstd_ready, e + 1)
                if e >= 2:
                    act.wait_ge(z_out[e % 2], 16 * NS * (e // 2))
                for j, (_, n) in enumerate(SLOTS):
                    ins = act.activation(z[0:n, e % 2, j, :], y[0:n, e % 2, j, :], ACT.Identity,
                                         bias=ynmr[0:n, e % 2, j:j + 1], scale=yrstd[0:n, e % 2, j:j + 1])
                ins.then_inc(z_ready, 1)

            ein_t(0)
            for e in range(E):
                for j in range(FC):
                    hidden(e, j)
                    if e >= 1 and j == 0:
                        split_high(4 * e + 3)
                    if e >= 1 and j == 1:
                        store_sums(e - 1)
                    if e >= 2 and j == 2:
                        norm_out(e - 2)
                    if e == E - 1 and j == 7:
                        norm_out(e - 1)
                    if e + 1 < E:
                        if j in (3, 4, 7):
                            split_high(4 * (e + 1) + (3, 4, 7).index(j))
                        if j == 5:
                            ein_t(e + 1)
            e = E - 1
            act.wait_ge(z_out[e % 2], 16 * NS * (e // 2))
            for j, (_, n) in enumerate(SLOTS):
                act.wait_ge(yrstd_ready, E + j)
                act.activation(z[0:n, e % 2, j, :], y[0:n, e % 2, j, :], ACT.Identity,
                               bias=ynmr[0:n, e % 2, j:j + 1], scale=yrstd[0:n, e % 2, j:j + 1]
                               ).then_inc(z_ready, 1)

        @block.vector
        def _(dve):
            steps = [0]

            def step(ins):
                steps[0] += 1
                ins.then_inc(dve_step, 1)

            def settle():
                dve.wait_ge(dve_step, steps[0])

            def link(ins):
                step(ins)
                settle()

            def make_gray(b):
                dve.wait_ge(red_ready, b + 1)
                if b == 2:
                    dve.wait_ge(first_out, 16)
                if b >= 2:
                    dve.wait_ge(gray_out[b % 2], 16 * (b // 2))
                link(dve.scalar_tensor_tensor(red[:, b % 2], pix[:, b % 2, 1], GRAY[1], red[:, b % 2],
                                              ALU.mult, ALU.add))
                dve.scalar_tensor_tensor(gray[:, b % 2, :, 1:D + 1], pix[:, b % 2, 2], GRAY[2], red[:, b % 2],
                                         ALU.mult, ALU.add).then_inc(gray_ready, 1)

            K = TAPS * GR
            dve.wait_ge(pool_const, 1)
            for s, (scaled, made) in enumerate(((first_red, first_gray), (red_ready, gray_ready))):
                dve.wait_ge(scaled, 1)
                link(dve.scalar_tensor_tensor(red[:, 0, s], pix[:, 0, 1, s], GRAY[1], red[:, 0, s],
                                              ALU.mult, ALU.add))
                dve.scalar_tensor_tensor(gray[:, 0, s, 1:D + 1], pix[:, 0, 2, s], GRAY[2], red[:, 0, s],
                                         ALU.mult, ALU.add).then_inc(made, 1)
            dve.wait_ge(taps_in, 16 * TAPS)
            dve.wait_ge(pool_const, 2)
            link(dve.tensor_scalar(half_taps[0:K], taps[0:K], 0.5, None, ALU.mult))
            for dy in range(TAPS):
                for f in range(2):
                    tap = (f * TAPS + dy) * TAPS
                    w = half_taps[0:K, tap:tap + 1]
                    if dy == 0:
                        ins = dve.tensor_scalar(band[0:K, f, :], tap_mask[0:K, dy, :], w, None, ALU.mult)
                    else:
                        ins = dve.scalar_tensor_tensor(band[0:K, f, :], tap_mask[0:K, dy, :], w,
                                                       band[0:K, f, :], ALU.mult, ALU.add)
                    if dy < TAPS - 1:
                        step(ins)
                    else:
                        ins.then_inc(band_ready, 1)
                settle()

            def residual_in(b, s):
                if s == 0:
                    dve.wait_ge(xnat_done, b + 1)
                if b == 0 and s == 0:
                    dve.wait_ge(consts_in, 32)
                ins = dve.tensor_tensor(xb[:, b % 2, s, :], bank[2][:, s * D:(s + 1) * D], bvb[:, :], ALU.add)
                step(ins) if s < SC - 1 else ins.then_inc(xb_ready, 1)

            def keys_low(b):
                dve.wait_ge(yT_hi_ready, b + 1)
                for c in range(DC):
                    ins = dve.scalar_tensor_tensor(yT_lo[:, c, :], bank[3][:, c * S:(c + 1) * S],
                                                   key_bias[:, c:c + 1], yT_hi[:, c, :].bitcast(F32),
                                                   ALU.add, ALU.subtract)
                    if c < DC - 1:
                        step(ins)
                ins.then_inc(yT_ready, 1)

            def softmax_max(b):
                dve.wait_ge(scores_done, b + 1)
                if b >= 1:
                    dve.wait_ge(probs_ready, b)
                for s in range(SC):
                    n = (s + 1) * P
                    dve.tensor_tensor_reduce(score[:, s, 0:n], bank[6][:, s * S:s * S + n],
                                             causal[:, S - n:S], -SCALE, -MASKED, ALU.add, ALU.min,
                                             nmax[:, s:s + 1]).then_inc(nmax_ready, 1)

            def softmax_sum(b):
                dve.wait_ge(probs_ready, b + 1)
                step(dve.reciprocal(rinv[:, b % 2, :], psumr[:, b % 2, :]))

            def attend(b):
                dve.wait_ge(attn_done, b + 1)
                settle()
                dve.wait_ge(xb_ready, b + 1)
                if b >= 2:
                    dve.wait_ge(t_ready, SC * (b - 1))
                for s in range(SC):
                    dve.scalar_tensor_tensor(resid[:, b % 2, s, :], bank[5][:, s * D:(s + 1) * D],
                                             rinv[:, b % 2, s:s + 1], xb[:, b % 2, s, :], ALU.mult, ALU.add
                                             ).then_inc(resid_ready, 1)
                for s in range(SC):
                    dve.wait_ge(resid_ready, SC * b + s + 1)
                    step(dve.bn_stats(stats[:, s, :], resid[:, b % 2, s, :]))
                if b >= 1:
                    dve.wait_ge(lone_scale_ready, b)
                settle()
                for s in range(SC):
                    step(dve.bn_aggr(mv[:, s, :], stats[:, s, :]))
                settle()
                step(dve.tensor_scalar(nmean[:, :], mv[:, :, 0], -1.0, None, ALU.mult))
                dve.tensor_scalar(ve[:, :], mv[:, :, 1], EPS, None, ALU.add).then_inc(var_ready, 1)

            def route(b):
                dve.wait_ge(logits_done, b + 1)
                logits = route_bank(b)[:, LOGITS:LOGITS + SC * E].rearrange("p (s e) -> p s e", e=E)
                link(dve.tensor_reduce(lmax[:, :], logits, AX_X, ALU.max))
                peak = lmax[:, :].unsqueeze(2).broadcast_to([P, SC, E])
                step(dve.tensor_tensor(hit[:, :, :], logits, peak, ALU.is_equal))
                dve.tensor_tensor(lsub[:, :, :], logits, peak, ALU.subtract).then_inc(lsub_ready, 1)
                settle()
                link(dve.tensor_tensor(hrank[:, :, :], hit[:, :, :], rank[:, :, :], ALU.mult))
                link(dve.tensor_reduce(best[:, b % 2], hrank[:, :, :], AX_X, ALU.max))
                dve.tensor_tensor(onehot[:, b % 2], rank[:, :, :],
                                  best[:, b % 2].unsqueeze(2).broadcast_to([P, SC, E]), ALU.is_equal
                                  ).then_inc(onehot_ready, 1)

            def tally(b):
                dve.wait_ge(onehot_ready, b + 1)
                link(dve.tensor_tensor(onehots[:, b + 1, :], onehots[:, b, :], onehot[:, b % 2, 0, :], ALU.add))
                link(dve.tensor_tensor(onehots[:, b + 1, :], onehots[:, b + 1, :], onehot[:, b % 2, 1, :],
                                       ALU.add))

            def factor(b):
                dve.wait_ge(lexp_ready, b + 1)
                link(dve.tensor_reduce(lsum[:, :], lexp[:, :, :], AX_X, ALU.add))
                dve.reciprocal(trow[:, b % TR, :, D], lsum[:, :]).then_inc(factor_ready, 1)

            def assign(b):
                dve.wait_ge(count_done, b + 1)
                dve.wait_ge(onehot_ready, b + 1)
                count = route_bank(b)[:, COUNTS:COUNTS + SC * E].rearrange("p (s e) -> p s e", e=E)
                step(dve.tensor_tensor(mine[:, :, :], onehot[:, b % 2], count, ALU.mult))
                step(dve.tensor_scalar(base[:, :], best[:, b % 2], -float(CAP), float(E * CAP - 1),
                                       ALU.mult, ALU.add))
                settle()
                link(dve.tensor_reduce(place[:, :], mine[:, :, :], AX_X, ALU.add))
                step(dve.tensor_scalar(over[:, :], place[:, :], float(CAP), float(NOWHERE), ALU.is_gt, ALU.mult))
                step(dve.tensor_tensor(basep[:, :], base[:, :], place[:, :], ALU.add))
                settle()
                if b >= TR:
                    dve.wait_ge(rows_out[b % TR], 16 * SC * (b // TR))
                dve.tensor_tensor(slot[:, b % TR, :], basep[:, :], over[:, :], ALU.add).then_inc(slot_ready, 1)

            dve.wait_ge(setup_mm, 2)
            link(dve.tensor_copy(wqk_hi.rearrange("p a b -> p (a b)"), bank[3][:, :]))
            dve.tensor_tensor(wqk_lo.rearrange("p a b -> p (a b)"), bank[3][:, :],
                              wqk_hi.bitcast(F32).rearrange("p a b -> p (a b)"), ALU.subtract
                              ).then_inc(setup_ev, 1)
            dve.wait_ge(wv_hi_ready, 1)
            for c in range(DC):
                step(dve.tensor_tensor(wvT_lo[:, c, 0:D], bank[2][:, c * D:(c + 1) * D],
                                       wvT_hi[:, c, 0:D].bitcast(F32), ALU.subtract))
            make_gray(1)
            dve.wait_ge(edges_ready, DC)
            dve.tensor_tensor(xT[:, 0], edges_abs[:, :, 0, :], edges_abs[:, :, 1, :], ALU.add
                              ).then_inc(xT_ready, 1)
            dve.wait_ge(xT_hi_ready, 1)
            dve.tensor_tensor(xT_lo[:, 0], xT[:, 0], xT_hi[:, 0].bitcast(F32), ALU.subtract
                              ).then_inc(xT_lo_ready, 1)
            dve.wait_ge(setup_mm, 3)
            biases = bank[4][:, DC:2 * DC].unsqueeze(2).broadcast_to([P, DC, VCOLS - D])
            step(dve.tensor_copy(wvT_hi[:, :, D:VCOLS], biases))
            step(dve.tensor_copy(key_bias[:, :], bank[4][:, 0:DC]))
            step(dve.tensor_scalar(bias_dot[:, :], bank[4][:, 2 * DC:2 * DC + 1], SCALE, None, ALU.mult))
            settle()
            dve.tensor_tensor(wvT_lo[:, :, D:VCOLS], biases, wvT_hi[:, :, D:VCOLS].bitcast(F32),
                              ALU.subtract).then_inc(setup_ev, 1)
            make_gray(2)
            dve.wait_ge(pool_const, 4)
            for i in range(L):
                keys_low(i)
                if i >= 2:
                    route(i - 2)
                if i >= 1:
                    attend(i - 1)
                if i >= 2:
                    factor(i - 2)
                    tally(i - 2)
                residual_in(i, 0)
                residual_in(i, 1)
                if i == 0:
                    make_gray(AHEAD_GRAY - 1)
                softmax_max(i)
                if i == L - 1:
                    keys_low(L)
                if i >= 2:
                    assign(i - 2)
                if i == 0:
                    softmax_sum(i)
                if i + AHEAD_GRAY < B:
                    make_gray(i + AHEAD_GRAY)
                if i >= 1:
                    softmax_sum(i)
            softmax_max(L)
            residual_in(L, 0)
            residual_in(L, 1)
            attend(L - 1)
            softmax_sum(L)
            attend(L)
            route(L - 2)
            tally(L - 2)
            factor(L - 2)
            route(L - 1)
            tally(L - 1)
            assign(L - 2)
            factor(L - 1)
            assign(L - 1)
            route(L)
            factor(L)
            assign(L)

            def split_low(n):
                e, k = divmod(n, 4)
                c = slice(k * PIECE, (k + 1) * PIECE)
                dve.wait_ge(w_hi_ready, n + 1)
                dve.tensor_tensor(w_lo[:, e % 2, c], w_raw[:, e % 2, c], w_hi[:, e % 2, c].bitcast(F32),
                                  ALU.subtract).then_inc(w_lo_ready, 1)

            def ein_t(e):
                for c, b in enumerate((3, 7)):
                    dve.wait_ge(einT_hi_ready, DC * e + c + 1)
                    ins = dve.tensor_tensor(einT_lo[:, e % 2, c, :], bank[b][:, 0:CAP],
                                            einT_hi[:, e % 2, c, :].bitcast(F32), ALU.subtract)
                    ins.then_inc(einT_ready, 1)

            def hidden(e, j):
                n = FC * e + j
                dve.wait_ge(h_hi_ready, n + 1)
                hi, lo = hidden_halves(n)
                dve.scalar_tensor_tensor(lo, bank[n % 2][:, 0:CAP], 0.0, hi.bitcast(F32), ALU.max, ALU.subtract
                                         ).then_inc(h_ready, 1)

            def expert_out(e):
                if e >= 2:
                    dve.wait_ge(z_ready, e - 1)
                dve.wait_ge(turned, e + 1)
                for j, (_, n) in enumerate(SLOTS):
                    at, o = TURNED[j]
                    dve.scalar_tensor_tensor(y[0:n, e % 2, j, :], bank[at][0:n, o:o + D],
                                             ein[0:n, e, j, D:D + 1], ein[0:n, e, j, 0:D],
                                             ALU.mult, ALU.add).then_inc(y_ready, 1)

            def expert_stats(e):
                for j, (_, n) in enumerate(SLOTS):
                    dve.wait_ge(y_ready, NS * e + j + 1)
                    step(dve.bn_stats(ystats[0:n, j, :], y[0:n, e % 2, j, :]))

            def expert_var(e):
                if e >= 1:
                    dve.wait_ge(yrstd_ready, e)
                settle()
                for j, (_, n) in enumerate(SLOTS):
                    step(dve.bn_aggr(ymv[0:n, j, :], ystats[0:n, j, :]))
                settle()
                step(dve.tensor_scalar(ynmean[:, :], ymv[:, :, 0], -1.0, None, ALU.mult))
                settle()
                dve.tensor_scalar(yve[:, :], ymv[:, :, 1], EPS, None, ALU.add).then_inc(yvar_ready, 1)

            dve.wait_ge(w_lo_ready, SPLIT_EARLY)
            for n in range(SPLIT_EARLY, 4):
                split_low(n)
            ein_t(0)
            for e in range(E):
                for j in range(FC):
                    hidden(e, j)
                    if e >= 1:
                        if j in (0, 1):
                            split_low(4 * e + 2 + j)
                        if j == 3:
                            expert_out(e - 1)
                        if j == (7 if e < E - 1 else 4):
                            expert_stats(e - 1)
                        if j == (7 if e < E - 1 else 5):
                            expert_var(e - 1)
                    if e + 1 < E:
                        if j in (4, 6):
                            split_low(4 * (e + 1) + (j - 4) // 2)
                        if j == 5:
                            ein_t(e + 1)
            e = E - 1
            dve.wait_ge(yrstd_ready, e)
            for j, (_, n) in enumerate(SLOTS):
                dve.wait_ge(last_done, j + 1)
                dve.scalar_tensor_tensor(y[0:n, e % 2, j, :], bank[LAST_BANKS[j]][0:n, 0:D],
                                         ein[0:n, e, j, D:D + 1], ein[0:n, e, j, 0:D],
                                         ALU.mult, ALU.add).then_inc(y_ready, 1)
                dve.wait_ge(y_ready, NS * e + j + 1)
                link(dve.bn_stats(ystats[0:n, j, :], y[0:n, e % 2, j, :]))
                link(dve.bn_aggr(ymv[0:n, j, :], ystats[0:n, j, :]))
                step(dve.tensor_scalar(ynmean[:, j:j + 1], ymv[:, j, 0:1], -1.0, None, ALU.mult))
                dve.tensor_scalar(yve[:, j:j + 1], ymv[:, j, 1:2], EPS, None, ALU.add).then_inc(yvar_ready, 1)
                settle()

        @block.tensor
        def _(pe):
            def product(to, a, b, first, last):
                (ah, al), (bh, bl) = a, b
                pe.matmul(to, ah, bh, start=first, stop=False)
                pe.matmul(to, ah, bl, start=False, stop=False)
                return pe.matmul(to, al, bh, start=False, stop=last)

            def setup():
                pe.wait_ge(attn_w_in, 16 * 3)
                pe.wait_ge(pool_const, 3)
                for c in range(DC):
                    for k in range(DC):
                        ins = pe.transpose(bank[2][:, c * D + k * P:c * D + (k + 1) * P],
                                           wv[:, k, c * P:(c + 1) * P], ident[:, :])
                ins.then_inc(setup_mm, 1)
                for c in range(DC):
                    for k in range(DC):
                        ins = pe.matmul(bank[3][:, c * D:(c + 1) * D], wq[:, k, c * P:(c + 1) * P],
                                        wk[:, k, :], start=(k == 0), stop=(k == DC - 1))
                ins.then_inc(setup_mm, 1)

            def setup_biases():
                pe.wait_ge(bias_in, 16 * 2)
                for c in range(DC):
                    for k in range(DC):
                        pe.matmul(bank[4][:, c:c + 1], wk[:, k, c * P:(c + 1) * P], bqc[:, k:k + 1],
                                  start=(k == 0), stop=(k == DC - 1))
                for c in range(DC):
                    for k in range(DC):
                        pe.matmul(bank[4][:, DC + c:DC + c + 1], wq[:, k, c * P:(c + 1) * P], bkc[:, k:k + 1],
                                  start=(k == 0), stop=(k == DC - 1))
                for k in range(DC):
                    ins = pe.matmul(bank[4][:, 2 * DC:2 * DC + 1], bqc[:, k:k + 1].broadcast_to([P, P]),
                                    bkc[:, k:k + 1], start=(k == 0), stop=(k == DC - 1))
                ins.then_inc(setup_mm, 1)

            def convolve_groups(b, c, first, end):
                K = TAPS * GR
                acc = bank[c][:, :].rearrange("p (f s) -> p f s", f=2)
                for g in range(first, end):
                    n = min(GO, S - g * GO)
                    ins = pe.matmul(acc[:, :, g * GO:g * GO + n], shifted[0:K, b % 2, g, c * P:(c + 1) * P],
                                    band[0:K, :, 0:n], start=True, stop=True)
                return ins

            def convolve(b):
                pe.wait_ge(shifted_in[b % 2], 16 * TAPS * (b // 2 + 1))
                for c in range(DC):
                    if b >= 1:
                        pe.wait_ge(edges_ready, DC * (b - 1) + c + 1)
                    convolve_groups(b, c, 0, GROUPS).then_inc(conv_done, 1)

            def project_keys(b):
                pe.wait_ge(xT_lo_ready, b + 1)
                if b >= 1:
                    pe.wait_ge(rowc_ready, b)
                for c in range(DC):
                    for k in range(DC):
                        w = slice(c * P, (c + 1) * P)
                        ins = product(bank[3][:, c * S:(c + 1) * S], (wqk_hi[:, k, w], wqk_lo[:, k, w]),
                                      (xT_hi[:, b % 2, k, :], xT_lo[:, b % 2, k, :]), k == 0, k == DC - 1)
                ins.then_inc(y_done, 1)

            def tokens_as_rows(b):
                if b >= 2:
                    pe.wait_ge(tT_ready, b - 1)
                for s in range(SC):
                    for c in range(DC):
                        ins = pe.transpose(bank[2][:, s * D + c * P:s * D + (c + 1) * P],
                                           xT[:, b % 2, c, s * P:(s + 1) * P], ident[:, :])
                ins.then_inc(xnat_done, 1)

            def project_values(b):
                pe.wait_ge(yT_ready, b + 1)
                for s, (at, o) in enumerate(((3, 0), (4, VALUES))):
                    if s == 1 and 2 <= b < L:
                        pe.wait_ge(lsub_ready, b - 1)
                    if b == 0:
                        pe.wait_ge(setup_ev, 2)
                    if s == 1 and b == L:
                        pe.wait_ge(slot_ready, b - 2)
                    t = slice(s * P, (s + 1) * P)
                    for k in range(DC):
                        ins = product(bank[at][:, o:o + VCOLS], (xT_hi[:, b % 2, k, t], xT_lo[:, b % 2, k, t]),
                                      (wvT_hi[:, k, :], wvT_lo[:, k, :]), k == 0, k == DC - 1)
                ins.then_inc(v_done, 1)

            def scores(b):
                if b >= 1:
                    pe.wait_ge(nmax_ready, SC * b)
                for s in range(SC):
                    n = (s + 1) * P
                    for k in range(DC):
                        q = slice(s * P, (s + 1) * P)
                        ins = product(bank[6][:, s * S:s * S + n], (yT_hi[:, k, q], yT_lo[:, k, q]),
                                      (xT_hi[:, b % 2, k, 0:n], xT_lo[:, b % 2, k, 0:n]), k == 0, k == DC - 1)
                ins.then_inc(scores_done, 1)

            def prob_t(b):
                pe.wait_ge(probs_ready, b + 1)
                pe.transpose(bank[7][:, 0:P], prob[:, 0, 0:P], ident[:, :])
                pe.transpose(bank[7][:, P:2 * P], prob[:, 1, 0:P], ident[:, :])
                pe.transpose(bank[7][:, 2 * P:3 * P], prob[:, 1, P:2 * P], ident[:, :]).then_inc(pT_done, 1)

            def attend(b):
                pe.wait_ge(probT_ready, b + 1)
                if b >= 1:
                    pe.wait_ge(resid_ready, SC * b)
                pe.matmul(bank[5][:, 0:D], probT[:, 0:P], val[:, b % 2, 0, :], start=True, stop=True)
                pe.matmul(bank[5][:, D:2 * D], probT[:, P:2 * P], val[:, b % 2, 0, :], start=True, stop=False)
                pe.matmul(bank[5][:, D:2 * D], probT[:, 2 * P:3 * P], val[:, b % 2, 1, :], start=False, stop=True
                          ).then_inc(attn_done, 1)

            def turn(b):
                pe.wait_ge(t_ready, SC * (b + 1))
                pe.wait_ge(xb_ready, min(b + 2, B))
                for c in range(DC):
                    for s in range(SC):
                        ins = pe.transpose(bank[2][:, c * S + s * P:c * S + (s + 1) * P],
                                           trow[:, b % TR, s, c * P:(c + 1) * P], ident[:, :])
                ins.then_inc(tT_done, 1)

            def logits(b):
                if b == 0:
                    pe.wait_ge(consts_in, 32)
                pe.wait_ge(tT_ready, b + 1)
                if b >= L - 1:
                    pe.wait_ge(edges_ready, DC * B)
                else:
                    if b >= 1:
                        pe.wait_ge(slot_ready, b)
                    pe.wait_ge(rowc_ready, b + 2 if b < L - 2 else B)
                for s in range(SC):
                    for k in range(DC):
                        o = LOGITS + s * E
                        ins = pe.matmul(route_bank(b)[:, o:o + E], tT[:, k, s * P:(s + 1) * P], wr[:, k, :],
                                        start=(k == 0), stop=(k == DC - 1))
                ins.then_inc(logits_done, 1)

            def count(b):
                pe.wait_ge(onehot_ready, b + 1)
                if b < L - 1:
                    pe.wait_ge(rowc_ready, min(b + 3, B))
                o, acc = COUNTS, route_bank(b)
                pe.matmul(acc[:, o:o + E], ones[:, :], onehots[:, b, :], start=True, stop=False)
                pe.matmul(acc[:, o:o + E], tri[:, :], onehot[:, b % 2, 0, :], start=False, stop=True)
                pe.matmul(acc[:, o + E:o + 2 * E], ones[:, :], onehots[:, b, :], start=True, stop=False)
                pe.matmul(acc[:, o + E:o + 2 * E], ones[:, :], onehot[:, b % 2, 0, :], start=False, stop=False)
                pe.matmul(acc[:, o + E:o + 2 * E], tri[:, :], onehot[:, b % 2, 1, :], start=False, stop=True
                          ).then_inc(count_done, 1)

            setup()
            pe.wait_ge(band_ready, 2)
            pe.wait_ge(first_shifted, 16 * TAPS)
            for c in range(DC):
                convolve_groups(0, c, 0, HALF_GROUPS)
            pe.wait_ge(shifted_in[0], 16 * TAPS)
            for c in range(DC):
                convolve_groups(0, c, HALF_GROUPS, GROUPS).then_inc(conv_done, 1)
            setup_biases()
            pe.wait_ge(setup_ev, 1)
            project_keys(0)
            for i in range(L):
                if i >= 1:
                    prob_t(i - 1)
                if 1 <= i:
                    project_keys(i)
                tokens_as_rows(i)
                if i >= 2:
                    logits(i - 2)
                if i >= 1:
                    attend(i - 1)
                project_values(i)
                scores(i)
                if i >= 2:
                    count(i - 2)
                if i == 0:
                    convolve(1)
                if i + AHEAD_CONV < B:
                    convolve(i + AHEAD_CONV)
                if i == L - 1:
                    project_keys(L)
                if i >= 1:
                    turn(i - 1)
            project_values(L)
            scores(L)
            prob_t(L - 1)
            tokens_as_rows(L)
            attend(L - 1)
            logits(L - 2)
            prob_t(L)
            attend(L)
            turn(L - 1)
            logits(L - 1)
            count(L - 2)
            turn(L)
            count(L - 1)
            logits(L)
            count(L)

            def ein_t(e):
                pe.wait_ge(ein_in[e], 32)
                if e >= 1:
                    pe.wait_ge(einT_ready, DC * e)
                for c, b in enumerate((3, 7)):
                    for j, (o, n) in enumerate(SLOTS):
                        ins = pe.transpose(bank[b][:, o:o + n], ein[0:n, e, j, c * P:(c + 1) * P],
                                           ident[0:n, 0:n])
                    ins.then_inc(einT_done, 1)

            def hidden(e, j):
                n = FC * e + j
                if j == 0:
                    pe.wait_ge(w_lo_ready, 4 * e + 2)
                if n >= 2:
                    pe.wait_ge(h_ready, n - 1)
                for k in range(DC):
                    if j == 0:
                        pe.wait_ge(einT_ready, DC * e + k + 1)
                    w = slice(k * F + j * P, k * F + (j + 1) * P)
                    ins = product(bank[n % 2][:, 0:CAP], (w_hi[:, e % 2, w], w_lo[:, e % 2, w]),
                                  (einT_hi[:, e % 2, k, :], einT_lo[:, e % 2, k, :]), k == 0, k == DC - 1)
                ins.then_inc(h_done, 1)

            def wait_hidden(e, j):
                pe.wait_ge(h_ready, FC * e + j + 1)
                if j % 4 == 0:
                    pe.wait_ge(w_lo_ready, 4 * e + 3 + j // 4)

            def halves_of_hidden(n, cols):
                return [half[:, cols] for half in hidden_halves(n)]

            def halves_of_second(e, first, end):
                return w_hi[:, e % 2, first:end], w_lo[:, e % 2, first:end]

            def expert_out(e, j):
                n = FC * e + j
                wait_hidden(e, j)
                w = DC * F + j * D
                for c in range(DC):
                    if j == 0 and e >= 1:
                        pe.wait_ge(sum_ready, DC * (e - 1) + c + 1)
                    ins = product(bank[SUM_BANKS[c]][:, 0:CAP], halves_of_second(e, w + c * P, w + (c + 1) * P),
                                  halves_of_hidden(n, slice(0, CAP)), j == 0, j == FC - 1)
                    if j == FC - 1 and c < DC - 1:
                        ins.then_inc(chunk_done, 1)
                ins.then_inc(h_used, 1)

            def turn_out(e):
                pe.wait_ge(sum_ready, DC * (e + 1))
                if e >= 1:
                    pe.wait_ge(y_ready, NS * e)
                for i, (o, m) in enumerate(SLOTS):
                    to, at = TURNED[i]
                    for c in range(DC):
                        ins = pe.transpose(bank[to][0:m, at + c * P:at + (c + 1) * P], sums[:, c, o:o + m],
                                           ident[:, :])
                ins.then_inc(turned, 1)

            def last_tile(i, j):
                o, m = SLOTS[i]
                w = DC * F + j * D
                ins = product(bank[LAST_BANKS[i]][0:m, 0:D], halves_of_hidden(FC * (E - 1) + j, slice(o, o + m)),
                              halves_of_second(E - 1, w, w + D), j == 0, j == FC - 1)
                if j == FC - 1:
                    ins.then_inc(last_done, 1)

            ein_t(0)
            for e in range(E):
                for j in range(FC):
                    hidden(e, j)
                    if j == 5 and e + 1 < E:
                        ein_t(e + 1)
                    n = FC * e + j - 2
                    if n >= FC * (E - 1):
                        wait_hidden(e, j - 2)
                        last_tile(0, j - 2)
                    elif n >= 0:
                        expert_out(n // FC, n % FC)
                    if j == 2 and e >= 1:
                        turn_out(e - 1)
            for j in range(FC - 2, FC):
                wait_hidden(E - 1, j)
                last_tile(0, j)
            pe.wait_ge(sum_ready, DC * (E - 1))
            for i in range(1, NS):
                for j in range(FC):
                    last_tile(i, j)


_INS = ['x', 'L0_tok_scharr', 'L0_attn_Wq', 'L0_attn_bq', 'L0_attn_Wk', 'L0_attn_bk', 'L0_attn_Wv', 'L0_attn_bv',
        'L0_ffn_Wr', 'L0_ffn_W1', 'L0_ffn_W2']
_OUTS = [((8, 256, 256), 'float32')]


def kernel(**inputs):
    import numpy as _np
    import concourse.bacc as _bacc
    from concourse import mybir as _mybir
    from concourse.bass_utils import run_bass_kernel_spmd as _run

    nc = _bacc.Bacc("TRN2", target_bir_lowering=False, num_devices=1)
    arrays, args = {}, []
    for name in _INS:
        a = _np.ascontiguousarray(inputs[name])
        arrays[f"in_{name}_dram"] = a
        args.append(nc.dram_tensor(f"in_{name}_dram", a.shape, _mybir.dt.from_np(a.dtype), kind="ExternalInput").ap())
    for i, (shape, dtype) in enumerate(_OUTS):
        dt = _mybir.dt.from_np(_np.dtype(dtype))
        args.append(nc.dram_tensor(f"out_{i}_dram", shape, dt, kind="ExternalOutput").ap())
    vit_tower_kernel(nc, *args)
    r = _run(nc, [arrays], core_ids=[0])
    got = tuple(r.results[0][f"out_{i}_dram"] for i in range(len(_OUTS)))
    return got[0]
```
